# Optimizing a Trainium2 kernel written in Bass

```python
import numpy as np
import jax
import jax.numpy as jnp

def _softmax(x, axis=-1):
    return jax.nn.softmax(x, axis=axis)

def _gelu(x):
    return jax.nn.gelu(x, approximate=True)

def _silu(x):
    return jax.nn.silu(x)

def _sigmoid(x):
    return jax.nn.sigmoid(x)

def _layernorm(x, axis=-1, eps=1e-05):
    m = jnp.mean(x, axis=axis, keepdims=True)
    v = jnp.var(x, axis=axis, keepdims=True)
    return (x - m) / jnp.sqrt(v + eps)

def _scatter_add(tgt, idx, src, axis=0):
    return tgt.at[idx].add(src)

def _segment_sum(src, seg, n):
    return jax.ops.segment_sum(src, seg, n)
kernel_name = 'mk_macaron_d1_jaxref_r8_ae5849'

def setup_inputs(seed: int=0):
    np.random.seed(seed)
    _w = jnp.asarray

    def _L0_attn_setup():
        import jax, jax.numpy as jnp
        import numpy as np
        C = 128
        T = 256
        B = 8
        key = jax.random.key(seed)
        k1, k2, k3 = jax.random.split(key, 3)
        x = jax.random.normal(k1, (B, T, C), dtype=jnp.float32)
        scale = 1.0 / np.sqrt(C)
        Wqkv = jax.random.normal(k2, (C, 3 * C), dtype=jnp.float32) * scale
        Wproj = jax.random.normal(k3, (C, C), dtype=jnp.float32) * scale
        return {'x': x, 'Wqkv': Wqkv, 'Wproj': Wproj}
    _L0_attn_in = _L0_attn_setup()

    def _L0_ffn_setup():
        import jax, jax.numpy as jnp
        import numpy as np
        DIM = 128
        DEPTH = 6
        HEADS = 16
        DIM_HEAD = 64
        WINDOW = 32
        INNER = HEADS * DIM_HEAD
        DIM_INNER = int(DIM * 4 * 2 / 3)
        QK_SCALE = 8.0

        def shift_tokens(t):
            a, s = jnp.split(t, 2, -1)
            s = jnp.pad(s, ((0, 0), (1, 0), (0, 0)))[:, :-1]
            return jnp.concatenate([a, s], -1)

        def l2norm(t):
            return t / jnp.maximum(jnp.linalg.norm(t, axis=-1, keepdims=True), 1e-12)

        def rotate_half(x):
            x1, x2 = jnp.split(x, 2, -1)
            return jnp.concatenate([-x2, x1], -1)

        def rotary_tables(n):
            half = jnp.arange(0, DIM_HEAD, 2, dtype=jnp.float32)
            inv_freq = 1.0 / 10000.0 ** (half / DIM_HEAD)
            t = jnp.arange(n, dtype=jnp.float32)
            freqs = t[:, None] * inv_freq[None, :]
            freqs = jnp.concatenate([freqs, freqs], -1)
            base_scale = (half + 0.4 * DIM_HEAD) / (1.4 * DIM_HEAD)
            power = (t - n // 2) / (WINDOW // 2)
            scale = base_scale[None, :] ** power[:, None]
            scale = jnp.concatenate([scale, scale], -1)
            return (freqs, scale)

        def local_attention(q, k, v):
            b, h, n, d = q.shape
            w = WINDOW
            nw = n // w
            bq = q.reshape(b, h, nw, w, d)
            bk = k.reshape(b, h, nw, w, d)
            bv = v.reshape(b, h, nw, w, d)

            def look(t):
                p = jnp.pad(t, ((0, 0), (0, 0), (1, 0), (0, 0), (0, 0)))
                return jnp.concatenate([p[:, :, :nw], p[:, :, 1:]], axis=3)
            bk2, bv2 = (look(bk), look(bv))
            seq = jnp.arange(n).reshape(nw, w)
            seq_p = jnp.pad(seq, ((1, 0), (0, 0)), constant_values=-1)
            jt = jnp.concatenate([seq_p[:nw], seq_p[1:]], axis=1)
            it = seq[:, :, None]
            jb = jt[:, None, :]
            mask = (it < jb) | (it > jb + w) | (jb == -1)
            sim = jnp.einsum('bhwie,bhwje->bhwij', bq, bk2) * QK_SCALE
            sim = jnp.where(mask, -jnp.finfo(sim.dtype).max, sim)
            attn = jax.nn.softmax(sim, -1)
            out = jnp.einsum('bhwij,bhwje->bhwie', attn, bv2)
            return out.reshape(b, h, n, d)

        def attn_layer(x, Wqkv, qs, ksc, Wo):
            b, n, _ = x.shape
            qkv = x @ Wqkv
            q, k, v = jnp.split(qkv, 3, -1)
            sh = lambda t: t.reshape(b, n, HEADS, DIM_HEAD).transpose(0, 2, 1, 3)
            q, k, v = (sh(q), sh(k), sh(v))
            q = l2norm(q) * qs
            k = l2norm(k) * ksc
            freqs, scale = rotary_tables(n)
            cos, sin = (jnp.cos(freqs), jnp.sin(freqs))
            q = q * cos * scale + rotate_half(q) * sin * scale
            inv = 1.0 / scale
            k = k * cos * inv + rotate_half(k) * sin * inv
            out = local_attention(q, k, v)
            out = out.transpose(0, 2, 1, 3).reshape(b, n, INNER)
            return out @ Wo

        def ffn_layer(x, g, bln, W1, b1, W2, b2):
            mu = x.mean(-1, keepdims=True)
            var = ((x - mu) ** 2).mean(-1, keepdims=True)
            xn = (x - mu) / jnp.sqrt(var + 1e-05) * g + bln
            hg = xn @ W1 + b1
            a, gate = jnp.split(hg, 2, -1)
            return a * jax.nn.gelu(gate, approximate=False) @ W2 + b2
        key = jax.random.key(seed)
        ks = jax.random.split(key, 8)
        B, N = (2, 256)
        init = lambda k, shape: jax.random.normal(k, shape, jnp.float32) * 0.02
        return {'x': jax.random.normal(ks[0], (B, N, DIM), jnp.float32), 'Wqkv': init(ks[1], (DEPTH, DIM, 3 * INNER)), 'q_scale': jnp.ones((DEPTH, DIM_HEAD), jnp.float32), 'k_scale': jnp.ones((DEPTH, DIM_HEAD), jnp.float32), 'Wo': init(ks[2], (DEPTH, INNER, DIM)), 'ln_g': jnp.ones((DEPTH, DIM), jnp.float32), 'ln_b': jnp.zeros((DEPTH, DIM), jnp.float32), 'W1': init(ks[3], (DEPTH, DIM, 2 * DIM_INNER)), 'b1': jnp.zeros((DEPTH, 2 * DIM_INNER), jnp.float32), 'W2': init(ks[4], (DEPTH, DIM_INNER, DIM)), 'b2': jnp.zeros((DEPTH, DIM), jnp.float32)}
    _L0_ffn_in = _L0_ffn_setup()
    _d = {'L0_attn_x': _L0_attn_in['x'], 'L0_attn_Wqkv': _L0_attn_in['Wqkv'], 'L0_attn_Wproj': _L0_attn_in['Wproj'], 'L0_ffn_Wqkv': _L0_ffn_in['Wqkv'], 'L0_ffn_q_scale': _L0_ffn_in['q_scale'], 'L0_ffn_k_scale': _L0_ffn_in['k_scale'], 'L0_ffn_Wo': _L0_ffn_in['Wo'], 'L0_ffn_ln_g': _L0_ffn_in['ln_g'], 'L0_ffn_ln_b': _L0_ffn_in['ln_b'], 'L0_ffn_W1': _L0_ffn_in['W1'], 'L0_ffn_b1': _L0_ffn_in['b1'], 'L0_ffn_W2': _L0_ffn_in['W2'], 'L0_ffn_b2': _L0_ffn_in['b2']}
    _x0 = _d['L0_attn_x']
    _d['L0_attn_x'] = jax.random.normal(jax.random.fold_in(jax.random.key(seed), 1), (1, 2048, 128), dtype=_x0.dtype)
    del _x0
    return _d

def reference(L0_attn_x, L0_attn_Wqkv, L0_attn_Wproj, L0_ffn_Wqkv, L0_ffn_q_scale, L0_ffn_k_scale, L0_ffn_Wo, L0_ffn_ln_g, L0_ffn_ln_b, L0_ffn_W1, L0_ffn_b1, L0_ffn_W2, L0_ffn_b2):

    def _L0_attn_ref(x, Wqkv, Wproj):
        import jax, jax.numpy as jnp
        import numpy as np
        C = 128
        T = 256
        B = 8
        t = x.shape[1]
        qkv = x @ Wqkv
        q, k, v = jnp.split(qkv, 3, axis=-1)
        w = jnp.einsum('btc,bsc->bts', q, k) * C ** (-0.5)
        causal = jnp.triu(jnp.ones((t, t), dtype=bool), k=1)
        w = jnp.where(causal, -jnp.inf, w)
        a = jax.nn.softmax(w, axis=-1)
        out = jnp.einsum('bts,bsc->btc', a, v)
        return out @ Wproj

    def _L0_ffn_ref(x, Wqkv, q_scale, k_scale, Wo, ln_g, ln_b, W1, b1, W2, b2):
        import jax, jax.numpy as jnp
        import numpy as np
        DIM = 128
        DEPTH = 6
        HEADS = 16
        DIM_HEAD = 64
        WINDOW = 32
        INNER = HEADS * DIM_HEAD
        DIM_INNER = int(DIM * 4 * 2 / 3)
        QK_SCALE = 8.0

        def shift_tokens(t):
            a, s = jnp.split(t, 2, -1)
            s = jnp.pad(s, ((0, 0), (1, 0), (0, 0)))[:, :-1]
            return jnp.concatenate([a, s], -1)

        def l2norm(t):
            return t / jnp.maximum(jnp.linalg.norm(t, axis=-1, keepdims=True), 1e-12)

        def rotate_half(x):
            x1, x2 = jnp.split(x, 2, -1)
            return jnp.concatenate([-x2, x1], -1)

        def rotary_tables(n):
            half = jnp.arange(0, DIM_HEAD, 2, dtype=jnp.float32)
            inv_freq = 1.0 / 10000.0 ** (half / DIM_HEAD)
            t = jnp.arange(n, dtype=jnp.float32)
            freqs = t[:, None] * inv_freq[None, :]
            freqs = jnp.concatenate([freqs, freqs], -1)
            base_scale = (half + 0.4 * DIM_HEAD) / (1.4 * DIM_HEAD)
            power = (t - n // 2) / (WINDOW // 2)
            scale = base_scale[None, :] ** power[:, None]
            scale = jnp.concatenate([scale, scale], -1)
            return (freqs, scale)

        def local_attention(q, k, v):
            b, h, n, d = q.shape
            w = WINDOW
            nw = n // w
            bq = q.reshape(b, h, nw, w, d)
            bk = k.reshape(b, h, nw, w, d)
            bv = v.reshape(b, h, nw, w, d)

            def look(t):
                p = jnp.pad(t, ((0, 0), (0, 0), (1, 0), (0, 0), (0, 0)))
                return jnp.concatenate([p[:, :, :nw], p[:, :, 1:]], axis=3)
            bk2, bv2 = (look(bk), look(bv))
            seq = jnp.arange(n).reshape(nw, w)
            seq_p = jnp.pad(seq, ((1, 0), (0, 0)), constant_values=-1)
            jt = jnp.concatenate([seq_p[:nw], seq_p[1:]], axis=1)
            it = seq[:, :, None]
            jb = jt[:, None, :]
            mask = (it < jb) | (it > jb + w) | (jb == -1)
            sim = jnp.einsum('bhwie,bhwje->bhwij', bq, bk2) * QK_SCALE
            sim = jnp.where(mask, -jnp.finfo(sim.dtype).max, sim)
            attn = jax.nn.softmax(sim, -1)
            out = jnp.einsum('bhwij,bhwje->bhwie', attn, bv2)
            return out.reshape(b, h, n, d)

        def attn_layer(x, Wqkv, qs, ksc, Wo):
            b, n, _ = x.shape
            qkv = x @ Wqkv
            q, k, v = jnp.split(qkv, 3, -1)
            sh = lambda t: t.reshape(b, n, HEADS, DIM_HEAD).transpose(0, 2, 1, 3)
            q, k, v = (sh(q), sh(k), sh(v))
            q = l2norm(q) * qs
            k = l2norm(k) * ksc
            freqs, scale = rotary_tables(n)
            cos, sin = (jnp.cos(freqs), jnp.sin(freqs))
            q = q * cos * scale + rotate_half(q) * sin * scale
            inv = 1.0 / scale
            k = k * cos * inv + rotate_half(k) * sin * inv
            out = local_attention(q, k, v)
            out = out.transpose(0, 2, 1, 3).reshape(b, n, INNER)
            return out @ Wo

        def ffn_layer(x, g, bln, W1, b1, W2, b2):
            mu = x.mean(-1, keepdims=True)
            var = ((x - mu) ** 2).mean(-1, keepdims=True)
            xn = (x - mu) / jnp.sqrt(var + 1e-05) * g + bln
            hg = xn @ W1 + b1
            a, gate = jnp.split(hg, 2, -1)
            return a * jax.nn.gelu(gate, approximate=False) @ W2 + b2
        for i in range(DEPTH):
            x = attn_layer(shift_tokens(x), Wqkv[i], q_scale[i], k_scale[i], Wo[i]) + x
            x = ffn_layer(shift_tokens(x), ln_g[i], ln_b[i], W1[i], b1[i], W2[i], b2[i]) + x
        return x
    x = L0_attn_x
    x = x + 0.5 * _L0_ffn_ref(_layernorm(x, axis=-1), L0_ffn_Wqkv, L0_ffn_q_scale, L0_ffn_k_scale, L0_ffn_Wo, L0_ffn_ln_g, L0_ffn_ln_b, L0_ffn_W1, L0_ffn_b1, L0_ffn_W2, L0_ffn_b2)
    x = x + _L0_attn_ref(_layernorm(x, axis=-1), L0_attn_Wqkv, L0_attn_Wproj)
    x = x + 0.5 * _L0_ffn_ref(_layernorm(x, axis=-1), L0_ffn_Wqkv, L0_ffn_q_scale, L0_ffn_k_scale, L0_ffn_Wo, L0_ffn_ln_g, L0_ffn_ln_b, L0_ffn_W1, L0_ffn_b1, L0_ffn_W2, L0_ffn_b2)
    return x

_drawn_inputs = setup_inputs


def setup_inputs(seed=0):
    import zlib

    import numpy as np

    out = dict(_drawn_inputs(seed))
    spreads = {'L0_ffn_q_scale': (1.0, 0.6),
     'L0_ffn_k_scale': (1.0, 0.6),
     'L0_ffn_ln_g': (1.0, 0.6),
     'L0_ffn_ln_b': (0.0, 0.8),
     'L0_ffn_b1': (0.0, 0.8),
     'L0_ffn_b2': (0.0, 0.1)}
    factors = {'L0_ffn_W1': 3.132, 'L0_ffn_W2': 3.059}
    for name, (base, spread) in spreads.items():
        noise = np.random.default_rng([zlib.crc32(name.encode()), seed]).standard_normal(out[name].shape)
        drawn = base * np.exp(spread * noise) if base else spread * noise
        out[name] = jnp.asarray(drawn.astype(out[name].dtype))
    for name, factor in factors.items():
        out[name] = (out[name] * factor).astype(out[name].dtype)
    return out
```

```python
from contextlib import ExitStack

import concourse.bass as bass
from concourse import mybir

F32 = mybir.dt.float32
BF16 = mybir.dt.bfloat16
I32 = mybir.dt.int32
ALU = mybir.AluOpType
ACT = mybir.ActivationFunctionType
AX_X = mybir.AxisListType.X

P = 128
TILE = 128
WINDOW = 32
DH = 64
PAIRS = 8
HALVES = 2
PPH = PAIRS // HALVES
HEADS_PER_HALF = 2 * PPH
BANK = 512
DEPTH = 6
HIDDEN = 341
HCH = [(0, 128), (128, 128), (256, HIDDEN - 256)]
QK_SCALE = 8.0
EPS = 1e-5
NEWTON = 3
ROOT_STEPS = 3 + 3 * NEWTON


def bass_macaron(nc, x_t, w_qkv, w_o, w_1, w_2, vecs, qk_scales, trig, rebase, mask, ident, causal,
                 a_wqkv, a_wproj, out_t):
    T = x_t.shape[1]
    TILES = T // TILE
    CHUNKS = T // BANK

    ctx = ExitStack()
    with ctx:
        def sb(name, shape, dt=F32):
            return ctx.enter_context(nc.sbuf_tensor(name, shape, dt))

        def sem(name):
            return ctx.enter_context(nc.semaphore(name))

        banks = [ctx.enter_context(nc.psum_tensor(f"bank{i}", [P, BANK], F32)) for i in range(8)]
        proj = banks[0:2]
        tran = banks[2:4]
        score = banks[4:6]
        outp = banks[6:8]

        wqkv = sb("wqkv", [P, 3 * PAIRS * P])
        wo = sb("wo", [P, PAIRS, P])
        w1 = sb("w1", [P, 2 * HIDDEN])
        w2 = sb("w2", [P, 3, P])
        vec = sb("vec", [P, 9])
        qks = sb("qks", [P, 4, DH])
        trig_sb = sb("trig_sb", [P, 4, TILES, DH])
        tab = sb("tab", [P, 4, TILES, DH])
        reb = sb("reb", [P, 1])
        maskb = sb("maskb", [P, 2, P], BF16)
        identb = sb("identb", [P, P], BF16)
        identf = sb("identf", [P, P])
        causalb = sb("causalb", [P, P], BF16)
        mean_w = sb("mean_w", [P, P])
        awqkv = sb("awqkv", [P, 3 * P])
        awproj = sb("awproj", [P, P])

        xm = sb("xm", [P, T])
        xT = sb("xT", [P, T])
        xA = sb("xA", [P, T + 1])
        xB = sb("xB", [P, T + 1])

        xq = sb("xq", [P, TILE])
        xv = sb("xv", [P, TILE])
        raw = sb("raw", [P, 2 * HALVES, BANK])
        sq = sb("sq", [P, HALVES, BANK])
        ssq = sb("ssq", [P, 2 * HALVES, HEADS_PER_HALF])
        root_s = sb("root_s", [P, 2 * HALVES * HEADS_PER_HALF])
        root_t = sb("root_t", [P, 2 * HALVES * HEADS_PER_HALF])
        rnorm = sb("rnorm", [P, 2 * HALVES, HEADS_PER_HALF])
        sinp = sb("sinp", [P, 2 * HALVES, BANK])
        qk = sb("qk", [P, 2 * HALVES, BANK])
        qz = sb("qz", [P, PAIRS, 4, 2, WINDOW])
        kT = sb("kT", [P, PAIRS, WINDOW + TILE])
        pb = sb("pb", [P, HALVES, BANK])
        mx = sb("mx", [P, HALVES, HEADS_PER_HALF])
        sm = sb("sm", [P, HALVES, HEADS_PER_HALF])
        rinv = sb("rinv", [P, HALVES, HEADS_PER_HALF])
        pT = sb("pT", [P, HALVES, PPH, P])
        v_area = sb("v_area", [P, 2 * HALVES, BANK])
        vt = v_area[:, 0:HALVES, :]
        vs = v_area[:, HALVES:, :]
        oT = sb("oT", [P, PAIRS, TILE])

        xc, xsq = raw[:, 0:2, :], raw[:, 2:4, :]
        xh, xn = sinp[:, 0:2, :], sinp[:, 2:4, :]
        rstd = sb("rstd", [P, BANK // P])
        ffn_area = sb("ffn_area", [P, 6, BANK])
        gate = ffn_area[:, 0:3, :]
        hid = ffn_area[:, 3:6, :]

        ld_const = sem("ld_const")
        ld_qkv, ld_o, ld_ffn, ld_scales = sem("ld_qkv"), sem("ld_o"), sem("ld_ffn"), sem("ld_scales")
        pe_tq, pe_tk, pe_tp = sem("pe_tq"), sem("pe_tk"), sem("pe_tp")
        pe_qk, pe_v, pe_s, pe_o, pe_y = (sem(s) for s in ("pe_qk", "pe_v", "pe_s", "pe_o", "pe_y"))
        act_qz, act_kt, act_pt = sem("act_qz"), sem("act_kt"), sem("act_pt")
        act_raw, act_sq, act_v, act_exp, act_o = (sem(s) for s in ("act_raw", "act_sq", "act_v", "act_exp", "act_o"))
        act_xq, act_xv = sem("act_xq"), sem("act_xv")
        dve_ssq, dve_cos, dve_rope, dve_halo = (sem(s) for s in ("dve_ssq", "dve_cos", "dve_rope", "dve_halo"))
        dve_max, dve_sub, dve_sum, dve_rinv, dve_y = (
            sem(s) for s in ("dve_max", "dve_sub", "dve_sum", "dve_rinv", "dve_y"))
        pool_sin, pool_qk, pool_pn, dve_xb = (sem(s) for s in ("pool_sin", "pool_qk", "pool_pn", "dve_xb"))
        pool_tab, pool_init, pool_vz = sem("pool_tab"), sem("pool_init"), sem("pool_vz")
        pool_held, dve_zero, dve_masks = sem("pool_held"), sem("dve_zero"), sem("dve_masks")
        root_done, f_root, n_root = sem("root_done"), sem("f_root"), sem("n_root")
        v_moved = [sem(f"v_moved{h}") for h in range(HALVES)]
        v_carried = sem("v_carried")
        f_mean, f_xc, f_sq, f_var, f_spread, f_xh, f_xn = (
            sem(s) for s in ("f_mean", "f_xc", "f_sq", "f_var", "f_spread", "f_xh", "f_xn"))
        f_gate, f_up, f_gelu, f_hid, f_down, f_x, f_shift = (
            sem(s) for s in ("f_gate", "f_up", "f_gelu", "f_hid", "f_down", "f_x", "f_shift"))
        n_mean, n_xc, n_sq, n_var, n_spread, n_x, n_shift = (
            sem(s) for s in ("n_mean", "n_xc", "n_sq", "n_var", "n_spread", "n_x", "n_shift"))
        h_x = sem("h_x")
        c_proj, c_evac, c_s, c_max, c_neg, c_exp, c_inv, c_t, c_pt, c_o, c_on, c_ot, c_otc, c_y, c_x = (
            sem(s) for s in ("c_proj", "c_evac", "c_s", "c_max", "c_neg", "c_exp", "c_inv", "c_t", "c_pt",
                             "c_o", "c_on", "c_ot", "c_otc", "c_y", "c_x"))
        out_done = sem("out_done")

        def heads(ap):
            return ap.rearrange("p (h d) -> p h d", d=DH)

        def per_head(ap):
            return ap.unsqueeze(2).broadcast_to([P, HEADS_PER_HALF, DH])

        def over_heads(ap, n=DH):
            return ap.unsqueeze(1).broadcast_to([P, HEADS_PER_HALF, n])

        def tile_steps(eng, step):
            step(0, None, None)
            step(1, 0, None)
            step(2, 1, 0)
            with eng.Fori(3, TILES) as a:
                step(a, a - 1, a - 2)
            step(None, TILES - 1, TILES - 2)
            step(None, None, TILES - 1)

        def glob(layer, t):
            return None if t is None else layer * TILES + t

        def tile_of(buf, t):
            return buf[:, t * TILE:(t + 1) * TILE] if isinstance(t, int) else buf[:, bass.ds(t * TILE, TILE)]

        CNT = CHUNKS

        def pe_attention(pe, L):
            def step(a, b, c):
                na, nb, nq = glob(L, a), glob(L, b), glob(L, c)
                if b is not None:
                    for h in range(HALVES):
                        pe.wait_ge(pool_qk, nb * 4 + (h + 1) + 1)
                        pe.wait_ge(act_kt, nb * 2 + 1)
                        if c is not None:
                            pe.wait_ge(act_pt, nq * 2 + 1)
                        for j in range(PPH):
                            last = nc.tensor.transpose(tran[h][:, j * P:(j + 1) * P],
                                                       qk[:, h, j * P:(j + 1) * P], identf[:, :])
                        last.then_inc(pe_tq, 1)
                if a is not None:
                    pe.wait_ge(act_xq, na + 2)
                    pe.wait_ge(act_sq, na * 4 + 1)
                    if c is not None:
                        pe.wait_ge(act_v, nq * 2 + 1)
                        pe.wait_ge(dve_y, nq + 1)
                    for h in range(HALVES):
                        nc.tensor.matmul(proj[h][:, :], xq[:, :], wqkv[:, h * BANK:(h + 1) * BANK],
                                         start=True, stop=True).then_inc(pe_qk, 1)
                if b is not None:
                    for h in range(HALVES):
                        pe.wait_ge(pool_qk, nb * 4 + (h + 3) + 1)
                        pe.wait_ge(act_qz, nb * 2 + (h + 1) + 1)
                        for j in range(PPH):
                            last = nc.tensor.transpose(tran[h][:, j * P:(j + 1) * P],
                                                       qk[:, 2 + h, j * P:(j + 1) * P], identf[:, :])
                        last.then_inc(pe_tk, 1)
                if a is not None:
                    for h in range(HALVES):
                        pe.wait_ge(act_sq, na * 4 + (h + 1) + 1)
                        nc.tensor.matmul(proj[h][:, :], xq[:, :],
                                         wqkv[:, PAIRS * P + h * BANK:PAIRS * P + (h + 1) * BANK],
                                         start=True, stop=True).then_inc(pe_qk, 1)
                if c is not None:
                    pe.wait_ge(act_xv, nq + 2)
                    for h in range(HALVES):
                        if a is not None:
                            pe.wait_ge(act_sq, na * 4 + (h + 3) + 1)
                        elif b is not None:
                            pe.wait_ge(act_sq, nb * 4 + 4 + 1)
                        if a is None:
                            pe.wait_ge(dve_y, nq + 1)
                            pe.wait_ge(act_v, nq * 2 + 1)
                        nc.tensor.matmul(proj[h][:, :], xv[:, :],
                                         wqkv[:, 2 * PAIRS * P + h * BANK:2 * PAIRS * P + (h + 1) * BANK],
                                         start=True, stop=True).then_inc(pe_v, 1)
                    for h in range(HALVES):
                        pe.wait_ge(pool_pn, nq * 2 + (h + 1) + 1)
                        if b is not None:
                            pe.wait_ge(act_kt, nb * 2 + (h + 1) + 1)
                        else:
                            pe.wait_ge(act_pt, nq * 2 + 1)
                        for j in range(PPH):
                            last = nc.tensor.transpose(tran[h][:, j * P:(j + 1) * P],
                                                       pb[:, h, j * P:(j + 1) * P], identf[:, :])
                        last.then_inc(pe_tp, 1)
                if b is not None:
                    first = 0 if (isinstance(b, int) and b == 0) else 1
                    pe.wait_ge(dve_halo, nb + 2)
                    pe.wait_ge(dve_sub, nb * 2 + 1)
                    if c is not None:
                        pe.wait_ge(act_o, nq * 2 + 1)
                    for h in range(HALVES):
                        pe.wait_ge(act_kt, nb * 2 + (h + 1) + 1)
                        nc.tensor.matmul(score[h][:, :].rearrange("p (j k) -> p j k", k=P), identb[:, :],
                                         maskb[:, first, :].unsqueeze(1).broadcast_to([P, PPH, P]),
                                         start=True, stop=False, skip_group_check=True)
                        for j in range(PPH):
                            for w in range(4):
                                u, wl = divmod(w, 2)
                                pr = h * PPH + j
                                last = nc.tensor.matmul(
                                    score[h][64 * wl:64 * wl + 64, j * P + u * 64:j * P + u * 64 + 64],
                                    qz[:, pr, w, :, :].rearrange("p a q -> p (a q)"),
                                    kT[:, pr, WINDOW * w:WINDOW * w + 64],
                                    start=False, stop=(j == PPH - 1 and w == 3), skip_group_check=True)
                        last.then_inc(pe_s, 1)
                if c is not None:
                    for h in range(HALVES):
                        dst = (outp, score)[h]
                        pe.wait_ge(act_pt, nq * 2 + (h + 1) + 1)
                        pe.wait_ge(act_v, nq * 2 + (h + 1) + 1)
                        pe.wait_ge(v_moved[h], (nq + 1) * 16)
                        if isinstance(c, int) and c == 0:
                            pe.wait_ge(pool_vz, L + 2)
                        else:
                            pe.wait_ge(v_carried, (L * (TILES - 1) + c) * 16)
                        pe.wait_ge(act_o, nq * 2 + 1)
                        if h == 1:
                            pe.wait_ge(dve_sub, (nq + (2 if b is not None else 1)) * 2 + 1)
                        for j in range(PPH):
                            for w in (0, 2, 1, 3):
                                u, wl = divmod(w, 2)
                                src = vt if wl else vs
                                last = nc.tensor.matmul(
                                    dst[u][:, (j * 2 + wl) * 64:(j * 2 + wl) * 64 + 64],
                                    src[64 * u:64 * u + 64, h, j * P:(j + 1) * P],
                                    pT[64 * u:64 * u + 64, h, j, 64 * wl:64 * wl + 64],
                                    start=True, stop=True, skip_group_check=True)
                        last.then_inc(pe_o, 1)
                    for h in range(HALVES):
                        pe.wait_ge(act_o, nq * 2 + (h + 1) + 1)
                        for j in range(PPH):
                            pr = h * PPH + j
                            last = nc.tensor.matmul(proj[0][:, 0:TILE], wo[:, pr, :], oT[:, pr, :],
                                                    start=(pr == 0), stop=(pr == PAIRS - 1))
                    last.then_inc(pe_y, 1)
            pe.wait_ge(ld_qkv, (L + 1) * 16)
            pe.wait_ge(ld_o, (L + 1) * 16)
            tile_steps(pe, step)

        def variance(squares):
            for m in range(BANK // P):
                last = nc.tensor.matmul(proj[0][:, m:m + 1], squares[:, m * P:(m + 1) * P], mean_w[:, 0:1],
                                        start=True, stop=True, skip_group_check=True)
            return last

        def spread_roots():
            for m in range(BANK // P):
                last = nc.tensor.matmul(proj[0][:, m * P:(m + 1) * P], rstd[:, m:m + 1].broadcast_to([P, P]),
                                        identf[:, :], start=True, stop=True, skip_group_check=True)
            return last

        def pe_ffn(pe, L):
            def mean(j):
                if j == 0:
                    pe.wait_ge(dve_y, (L + 1) * TILES + 1)
                    pe.wait_ge(dve_xb, (L + 1) * TILES + 1)
                else:
                    pe.wait_ge(f_xh, L * CNT + j + 1)
                nc.tensor.matmul(proj[0][:, :], mean_w[:, :], xB[:, j * BANK:(j + 1) * BANK],
                                 start=True, stop=True).then_inc(f_mean, 1)

            def var(j):
                pe.wait_ge(f_sq, L * CNT + j + 2)
                variance(xsq[:, j % 2, :]).then_inc(f_var, 1)

            def spread(j):
                pe.wait_ge(f_root, (L * CNT + j + 1) * ROOT_STEPS + 1)
                spread_roots().then_inc(f_spread, 1)

            def up(j, k):
                off, n = HCH[k]
                pe.wait_ge(f_xn, L * CNT + j + 2)
                pe_bank = banks[2 + 2 * k], banks[3 + 2 * k]
                if j > 0:
                    pe.wait_ge(f_hid, (L * CNT + j - 1) * 3 + k + 2)
                nc.tensor.matmul(pe_bank[1][0:n, :], w1[:, HIDDEN + off:HIDDEN + off + n], xn[:, j % 2, :],
                                 start=True, stop=True).then_inc(f_gate, 1)
                nc.tensor.matmul(pe_bank[0][0:n, :], w1[:, off:off + n], xn[:, j % 2, :],
                                 start=True, stop=True).then_inc(f_up, 1)

            def down(j):
                pe.wait_ge(f_x, L * CNT + j + 1)
                for k, (off, n) in enumerate(HCH):
                    pe.wait_ge(f_hid, (L * CNT + j) * 3 + k + 2)
                    last = nc.tensor.matmul(proj[1][:, :], w2[0:n, k, :], hid[0:n, k, :],
                                            start=(k == 0), stop=(k == 2))
                last.then_inc(f_down, 1)

            pe.wait_ge(ld_ffn, (L + 1) * 64)
            mean(0)
            var(0)
            spread(0)
            for j in range(CHUNKS):
                if j + 1 < CHUNKS:
                    mean(j + 1)
                up(j, 0)
                if j + 1 < CHUNKS:
                    var(j + 1)
                up(j, 1)
                if j + 1 < CHUNKS:
                    spread(j + 1)
                up(j, 2)
                down(j)

        def act_attention(act, L):
            def step(a, b, c):
                na, nb, nq = glob(L, a), glob(L, b), glob(L, c)
                def parts(kind):
                    for e in (2 * kind, 2 * kind + 1):
                        act.wait_ge(pe_qk, na * 4 + (e + 1) + 1)
                        act.wait_ge(pool_sin, na * 4 + 1)
                        act.wait_ge(dve_cos, na * 4 + 1)
                        nc.scalar.activation(raw[:, e, :], proj[e % 2][:, :], ACT.Copy).then_inc(act_raw, 1)
                        act.wait_ge(dve_ssq, na * 4 + max(0, e - 1) + 1)
                        nc.scalar.activation(sq[:, e % 2, :], proj[e % 2][:, :], ACT.Square).then_inc(act_sq, 1)

                if a is not None:
                    act.wait_ge(pe_qk, na * 4 + 1)
                    nc.scalar.activation(xq[:, :], tile_of(xA, a), ACT.Copy).then_inc(act_xq, 1)
                if c is not None:
                    act.wait_ge(pe_v, nq * 2 + 1)
                    nc.scalar.activation(xv[:, :], tile_of(xA, c), ACT.Copy).then_inc(act_xv, 1)
                if b is not None:
                    for h in range(HALVES):
                        act.wait_ge(pe_tq, nb * 2 + (h + 1) + 1)
                        act.wait_ge(pe_s, nb * 2 + 1)
                        for e in range(2):
                            last = nc.scalar.activation(
                                qz[64 * e:64 * e + 64, h * PPH:(h + 1) * PPH, :, e, :],
                                tran[h][64 * e:64 * e + 64, :].rearrange("p (j w q) -> p j w q", w=4, q=WINDOW),
                                ACT.Copy)
                        last.then_inc(act_qz, 1)
                if a is not None:
                    parts(0)
                if b is not None:
                    act.wait_ge(dve_halo, nb + 2)
                    for h in range(HALVES):
                        act.wait_ge(pe_tk, nb * 2 + (h + 1) + 1)
                        nc.scalar.activation(kT[:, h * PPH:(h + 1) * PPH, WINDOW:],
                                             tran[h][:, :].rearrange("p (j t) -> p j t", t=TILE),
                                             ACT.Copy).then_inc(act_kt, 1)
                if a is not None:
                    parts(1)
                if c is not None:
                    act.wait_ge(pe_o, nq * 2 + 1)
                    if not (isinstance(c, int) and c == 0):
                        act.wait_ge(v_carried, (L * (TILES - 1) + c) * 16)
                    for h in range(HALVES):
                        act.wait_ge(pe_v, nq * 2 + (h + 1) + 1)
                        nc.scalar.activation(vt[:, h, :], proj[h][:, :], ACT.Copy).then_inc(act_v, 1)
                    for h in range(HALVES):
                        act.wait_ge(pe_tp, nq * 2 + (h + 1) + 1)
                        nc.scalar.activation(pT[:, h, :, :].rearrange("p j q -> p (j q)"), tran[h][:, :],
                                             ACT.Copy).then_inc(act_pt, 1)
                if b is not None:
                    for h in range(HALVES):
                        act.wait_ge(dve_sub, nb * 2 + (h + 1) + 1)
                        nc.scalar.activation(pb[:, h, :], pb[:, h, :], ACT.Exp, scale=QK_SCALE)\
                            .then_inc(act_exp, 1)
                if c is not None:
                    act.wait_ge(pe_y, nq + 1)
                    for h in range(HALVES):
                        src = (outp, score)[h]
                        act.wait_ge(pe_o, nq * 2 + (h + 1) + 1)
                        for e in range(2):
                            for u in range(2):
                                last = nc.scalar.activation(
                                    oT[64 * e:64 * e + 64, h * PPH:(h + 1) * PPH, 64 * u:64 * u + 64]
                                    .rearrange("p j (w q) -> p j w q", q=WINDOW),
                                    src[u][64 * e:64 * e + 64, :]
                                    .rearrange("p (j w e q) -> p j w e q", w=2, e=2, q=WINDOW)[:, :, :, e, :],
                                    ACT.Copy)
                        last.then_inc(act_o, 1)
            act.wait_ge(f_shift, L * CNT + 1)
            tile_steps(act, step)

        def act_ffn(act, L):
            act.wait_ge(ld_ffn, (L + 1) * 64)
            def square(j):
                act.wait_ge(f_xc, L * CNT + j + 2)
                if j >= 2:
                    act.wait_ge(f_var, L * CNT + j - 1 + 1)
                nc.scalar.activation(xsq[:, j % 2, :], xc[:, j % 2, :], ACT.Square).then_inc(f_sq, 1)
            square(0)
            for j in range(CHUNKS):
                if j + 1 < CHUNKS:
                    square(j + 1)
                for k, (off, n) in enumerate(HCH):
                    act.wait_ge(f_gate, (L * CNT + j) * 3 + k + 2)
                    if j > 0:
                        act.wait_ge(f_hid, (L * CNT + j - 1) * 3 + k + 2)
                    nc.scalar.activation(gate[0:n, k, :], banks[3 + 2 * k][0:n, :], ACT.Gelu,
                                         bias=vec[0:n, 6 + k:7 + k]).then_inc(f_gelu, 1)

        def shift(dst, src, start, n):
            if isinstance(start, int):
                now, later = slice(start, start + n), slice(start + 1, start + 1 + n)
            else:
                now, later = bass.ds(start, n), bass.ds(start + 1, n)
            nc.vector.tensor_copy(dst[0:64, now], src[0:64, now])
            return nc.vector.tensor_copy(dst[64:P, later], src[64:P, now])

        def inverse_root(dve, src, floor, floor_op, y, done, base):
            w = src.shape[1]
            s_, t_ = root_s[:, 0:w], root_t[:, 0:w]
            nc.vector.tensor_scalar(s_, src, floor, None, floor_op).then_inc(done, 1)
            dve.wait_ge(done, base + 1)
            nc.vector.tensor_scalar(t_.bitcast(I32), s_.bitcast(I32), 1, None, ALU.arith_shift_right)\
                .then_inc(done, 1)
            dve.wait_ge(done, base + 2)
            nc.vector.tensor_scalar(y.bitcast(I32), t_.bitcast(I32), -1.0, float(0x5f3759df), ALU.mult, ALU.add)\
                .then_inc(done, 1)
            for i in range(NEWTON):
                dve.wait_ge(done, base + 3 + 3 * i)
                nc.vector.tensor_tensor(t_, y, y, ALU.mult).then_inc(done, 1)
                dve.wait_ge(done, base + 4 + 3 * i)
                nc.vector.scalar_tensor_tensor(t_, t_, -0.5, s_, ALU.mult, ALU.mult).then_inc(done, 1)
                dve.wait_ge(done, base + 5 + 3 * i)
                nc.vector.scalar_tensor_tensor(y, t_, 1.5, y, ALU.add, ALU.mult).then_inc(done, 1)

        def dve_attention(dve, L):
            def table(i, t):
                return tab[:, i, t, :] if isinstance(t, int) else \
                    tab[:, i, bass.ds(t, 1), :].rearrange("p a d -> p (a d)")

            def cosine_and_sums(t, n, e):
                dve.wait_ge(act_raw, n * 4 + (e + 1) + 1)
                dve.wait_ge((pe_tq, pe_tk)[e // 2], n * 2 + 1)
                nc.vector.tensor_tensor(heads(qk[:, e, :]), heads(raw[:, e, :]), over_heads(table(e // 2 * 2, t)),
                                        ALU.mult).then_inc(dve_cos, 1)
                dve.wait_ge(act_sq, n * 4 + (e + 1) + 1)
                nc.vector.tensor_reduce(ssq[:, e, :], heads(sq[:, e % 2, :]), AX_X, ALU.add).then_inc(dve_ssq, 1)

            def rotate(n, e):
                dve.wait_ge(pool_sin, n * 4 + (e + 1) + 1)
                dve.wait_ge(dve_cos, n * 4 + (e + 1) + 1)
                nc.vector.tensor_tensor(qk[:, e, :], qk[:, e, :], sinp[:, e, :], ALU.add).then_inc(dve_rope, 1)

            def step(a, b, c):
                na, nb, nq = glob(L, a), glob(L, b), glob(L, c)
                if b is not None:
                    dve.wait_ge(pe_s, nb * 2 + 1)
                    if isinstance(b, int) and b == 0:
                        nc.vector.memset(kT[:, :, 0:WINDOW], 0.0).then_inc(dve_halo, 1)
                    else:
                        dve.wait_ge(act_kt, nb * 2 + 1)
                        nc.vector.tensor_scalar(kT[:, :, 0:WINDOW], kT[:, :, TILE:TILE + WINDOW], reb[:, 0:1], None,
                                                ALU.mult).then_inc(dve_halo, 1)
                if a is not None:
                    for e in range(4):
                        cosine_and_sums(a, na, e)
                    rotate(na, 0)
                    rotate(na, 1)
                    dve.wait_ge(dve_ssq, na * 4 + 4 + 1)
                    dve.wait_ge(pool_qk, na * 4 + 1)
                    inverse_root(dve, ssq[:, :, :].rearrange("p e h -> p (e h)"), 1e-24, ALU.max,
                                 rnorm[:, :, :].rearrange("p e h -> p (e h)"), root_done, na * ROOT_STEPS + 1)
                    rotate(na, 2)
                    rotate(na, 3)
                if b is not None:
                    for h in range(HALVES):
                        dve.wait_ge(pe_s, nb * 2 + (h + 1) + 1)
                        dve.wait_ge(dve_sub, nb * 2 + 1)
                        nc.vector.tensor_reduce(mx[:, h, :], heads(score[h][:, :]), AX_X, ALU.max)\
                            .then_inc(dve_max, 1)
                        dve.wait_ge(dve_max, nb * 2 + (h + 1) + 1)
                        dve.wait_ge(pe_tp, nb * 2 + 1)
                        nc.vector.tensor_tensor(heads(pb[:, h, :]), heads(score[h][:, :]), per_head(mx[:, h, :]),
                                                ALU.subtract).then_inc(dve_sub, 1)
                    for h in range(HALVES):
                        dve.wait_ge(act_exp, nb * 2 + (h + 1) + 1)
                        dve.wait_ge(dve_rinv, nb * 2 + 1)
                        nc.vector.tensor_reduce(sm[:, h, :], heads(pb[:, h, :]), AX_X, ALU.add)\
                            .then_inc(dve_sum, 1)
                        dve.wait_ge(dve_sum, nb * 2 + (h + 1) + 1)
                        dve.wait_ge(pool_pn, nb * 2 + 1)
                        nc.vector.reciprocal(rinv[:, h, :], sm[:, h, :]).then_inc(dve_rinv, 1)
                if c is not None:
                    dve.wait_ge(pe_y, nq + 2)
                    xt = tile_of(xT, c)
                    nc.vector.tensor_tensor(xt, proj[0][:, 0:TILE], xt, ALU.add).then_inc(dve_y, 1)
                    dve.wait_ge(dve_y, nq + 2)
                    shift(xB, xT, c * TILE, TILE).then_inc(dve_xb, 1)
            dve.wait_ge(pool_tab, L + 2)
            tile_steps(dve, step)

        def dve_ffn(dve, L):
            dve.wait_ge(ld_ffn, (L + 1) * 64)
            def centre(j):
                dve.wait_ge(f_mean, L * CNT + j + 2)
                if j >= 2:
                    dve.wait_ge(f_xh, L * CNT + j - 1 + 1)
                    dve.wait_ge(f_sq, L * CNT + j - 1 + 1)
                nc.vector.tensor_tensor(xc[:, j % 2, :], xB[:, j * BANK:(j + 1) * BANK], proj[0][:, :],
                                        ALU.subtract).then_inc(f_xc, 1)

            def root(j):
                dve.wait_ge(f_var, L * CNT + j + 2)
                inverse_root(dve, proj[0][:, 0:BANK // P], EPS, ALU.add, rstd[:, :], f_root,
                             (L * CNT + j) * ROOT_STEPS + 1)

            def norm(j):
                dve.wait_ge(f_spread, L * CNT + j + 2)
                if j >= 2:
                    dve.wait_ge(f_xn, L * CNT + j - 1 + 1)
                nc.vector.tensor_tensor(xh[:, j % 2, :], xc[:, j % 2, :], proj[0][:, :], ALU.mult)\
                    .then_inc(f_xh, 1)
                dve.wait_ge(f_xh, L * CNT + j + 2)
                if j >= 2:
                    dve.wait_ge(f_up, (L * CNT + j - 1) * 3 + 1)
                nc.vector.tensor_scalar(xn[:, j % 2, :], xh[:, j % 2, :], vec[:, 0:1], vec[:, 1:2],
                                        ALU.mult, ALU.add).then_inc(f_xn, 1)

            centre(0)
            root(0)
            norm(0)
            for j in range(CHUNKS):
                if j + 1 < CHUNKS:
                    centre(j + 1)
                for k, (off, n) in enumerate(HCH):
                    dve.wait_ge(f_up, (L * CNT + j) * 3 + k + 2)
                    dve.wait_ge(f_gelu, (L * CNT + j) * 3 + k + 2)
                    if j > 0:
                        dve.wait_ge(f_down, L * CNT + j + 1)
                    nc.vector.scalar_tensor_tensor(hid[0:n, k, :], banks[2 + 2 * k][0:n, :], vec[0:n, 3 + k:4 + k],
                                                   gate[0:n, k, :], ALU.add, ALU.mult).then_inc(f_hid, 1)
                    if k == 0 and j + 1 < CHUNKS:
                        root(j + 1)
                    if k == 1 and j + 1 < CHUNKS:
                        norm(j + 1)
                dve.wait_ge(f_down, L * CNT + j + 2)
                xt = xT[:, j * BANK:(j + 1) * BANK]
                nc.vector.scalar_tensor_tensor(xt, proj[1][:, :], vec[:, 2:3], xt, ALU.add, ALU.add)\
                    .then_inc(f_x, 1)
                dve.wait_ge(f_x, L * CNT + j + 2)
                shift(xA, xT, j * BANK, BANK).then_inc(f_shift, 1)

        def hold(pool):
            pool.sem_inc(pool_held, 1)

        def fold_scales(pool, k):
            pool.wait_ge(ld_scales, (k + 1) * 16)
            hold(pool)
            for i in range(4):
                last = nc.gpsimd.tensor_tensor(tab[:, i, :, :], trig_sb[:, i, :, :],
                                               qks[:, i, :].unsqueeze(1).broadcast_to([P, TILES, DH]), ALU.mult)
            last.then_inc(pool_tab, 1)

        def pool_attention(pool, L):
            def sine(t, n, e):
                pool.wait_ge(act_raw, n * 4 + (e + 1) + 1)
                pool.wait_ge(dve_rope, n * 4 + 1)
                i = e // 2 * 2 + 1
                tb = tab[:, i, t, :] if isinstance(t, int) else \
                    tab[:, i, bass.ds(t, 1), :].rearrange("p a d -> p (a d)")
                half = DH // 2
                hold(pool)
                for o in range(2):
                    last = nc.gpsimd.tensor_tensor(
                        heads(sinp[:, e, :])[:, :, o * half:(o + 1) * half],
                        heads(raw[:, e, :])[:, :, (1 - o) * half:(2 - o) * half],
                        over_heads(tb[:, o * half:(o + 1) * half], half), ALU.mult)
                last.then_inc(pool_sin, 1)

            def step(a, b, c):
                na, nb, nq = glob(L, a), glob(L, b), glob(L, c)
                if a is not None:
                    for e in range(4):
                        sine(a, na, e)
                    for e in range(4):
                        pool.wait_ge(dve_rope, na * 4 + (e + 1) + 1)
                        pool.wait_ge(root_done, (na + 1) * ROOT_STEPS + 1)
                        hold(pool)
                        nc.gpsimd.tensor_tensor(heads(qk[:, e, :]), heads(qk[:, e, :]), per_head(rnorm[:, e, :]),
                                                ALU.mult).then_inc(pool_qk, 1)
                if isinstance(b, int) and b == 0:
                    pool.wait_ge(pe_o, nb * 2 + 1)
                    hold(pool)
                    nc.gpsimd.memset(vs[:, :, :], 0.0).then_inc(pool_vz, 1)
                if b is not None:
                    for h in range(HALVES):
                        pool.wait_ge(dve_rinv, nb * 2 + (h + 1) + 1)
                        hold(pool)
                        nc.gpsimd.tensor_tensor(heads(pb[:, h, :]), heads(pb[:, h, :]), per_head(rinv[:, h, :]),
                                                ALU.mult).then_inc(pool_pn, 1)
            pool.wait_ge(pool_tab, L + 2)
            tile_steps(pool, step)

        def pool_ffn(pool, L):
            pool.wait_ge(dve_cos, (L + 1) * TILES * 4 + 1)
            fold_scales(pool, L + 1)

        def sp_layer(sp, L, l):
            sp.wait_ge(f_down, L * CNT + 1)
            sp.wait_ge(f_x, L * CNT + 1)
            sp.dma_start(w1[:, :], w_1[bass.ds(l, 1), :, :].rearrange("a c h -> (a c) h")).then_inc(ld_ffn, 16)
            sp.dma_start(w2[:, 0:2, :], w_2[bass.ds(l, 1), 0:256, :].rearrange("a (k r) c -> r (a k) c", r=P))\
                .then_inc(ld_ffn, 16)
            sp.dma_start(w2[0:HIDDEN - 256, 2, :], w_2[bass.ds(l, 1), 256:HIDDEN, :].rearrange("a r c -> (a r) c"))\
                .then_inc(ld_ffn, 16)
            sp.dma_start(vec[:, :], vecs[bass.ds(l, 1), :, :].rearrange("a p v -> (a p) v")).then_inc(ld_ffn, 16)
            sp.wait_ge(pool_tab, L + 2)
            sp.dma_start(qks[:, :, :], qk_scales[bass.ds(l + 1, 1), :, :].rearrange("a i d -> a (i d)")
                         .broadcast_to([P, 4 * DH]).rearrange("p (i d) -> p i d", d=DH)).then_inc(ld_scales, 16)

            def step(a, b, c):
                if c is None:
                    return
                nq = glob(L, c)
                if isinstance(c, int) and c == 0:
                    sp.wait_ge(pool_vz, L + 2)
                for h in range(HALVES):
                    sp.wait_ge(act_v, nq * 2 + (h + 1) + 1)
                    sp.dma_start(vs[WINDOW:P, h, :], vt[0:P - WINDOW, h, :]).then_inc(v_moved[h], 16)
                if not (isinstance(c, int) and c == TILES - 1):
                    sp.wait_ge(pe_o, nq * 2 + 2 + 1)
                    sp.dma_start(vs[0:WINDOW, :, :], vt[P - WINDOW:P, :, :]).then_inc(v_carried, 16)
            tile_steps(sp, step)
            sp.wait_ge(pe_v, (L + 1) * TILES * 2 + 1)
            sp.dma_start(wqkv[:, :], w_qkv[bass.ds(l + 1, 1), :, :].rearrange("a c n -> (a c) n"))\
                .then_inc(ld_qkv, 16)
            sp.wait_ge(pe_y, (L + 1) * TILES + 1)
            sp.dma_start(wo[:, :, :], w_o[bass.ds(l + 1, 1), :, :].rearrange("a (j r) c -> r (a j) c", r=P))\
                .then_inc(ld_o, 16)

        def pe_norm(pe, blk):
            for j in range(CHUNKS):
                n = blk * CHUNKS + j
                pe.wait_ge(n_x, n + 1)
                if blk == 0:
                    pe.wait_ge(ld_const, LOADS * 16)
                    pe.wait_ge(pool_init, 1 + 1)
                elif blk == 1:
                    pe.wait_ge(h_x, j + 2)
                    pe.wait_ge(f_xh, DEPTH * CNT + 1)
                else:
                    pe.wait_ge(c_x, TILES + 1)
                nc.tensor.matmul(proj[0][:, :], mean_w[:, :], xm[:, j * BANK:(j + 1) * BANK],
                                 start=True, stop=True).then_inc(n_mean, 1)
                pe.wait_ge(n_sq, n + 2)
                variance(xsq[:, 0, :]).then_inc(n_var, 1)
                pe.wait_ge(n_root, (n + 1) * ROOT_STEPS + 1)
                spread_roots().then_inc(n_spread, 1)

        def act_norm(act, blk):
            for j in range(CHUNKS):
                n = blk * CHUNKS + j
                act.wait_ge(n_xc, n + 2)
                nc.scalar.activation(xsq[:, 0, :], xc[:, 0, :], ACT.Square).then_inc(n_sq, 1)

        def dve_norm(dve, blk):
            for j in range(CHUNKS):
                n = blk * CHUNKS + j
                dve.wait_ge(n_mean, n + 2)
                dve.wait_ge(n_x, n + 1)
                nc.vector.tensor_tensor(xc[:, 0, :], xm[:, j * BANK:(j + 1) * BANK], proj[0][:, :],
                                        ALU.subtract).then_inc(n_xc, 1)
                dve.wait_ge(n_var, n + 2)
                inverse_root(dve, proj[0][:, 0:BANK // P], EPS, ALU.add, rstd[:, :], n_root, n * ROOT_STEPS + 1)
                dve.wait_ge(n_spread, n + 2)
                nc.vector.tensor_tensor(xT[:, j * BANK:(j + 1) * BANK], xc[:, 0, :], proj[0][:, :], ALU.mult)\
                    .then_inc(n_x, 1)
                if blk != 1:
                    dve.wait_ge(n_x, n + 2)
                    shift(xA, xT, j * BANK, BANK).then_inc(n_shift, 1)

        def dve_half_step(dve, blk):
            dve.wait_ge(f_x, (blk + 1) * DEPTH * CNT + 1)
            for j in range(CHUNKS):
                s = slice(j * BANK, (j + 1) * BANK)
                nc.vector.scalar_tensor_tensor(xm[:, s], xT[:, s], 0.5, xm[:, s], ALU.mult, ALU.add)\
                    .then_inc(h_x, 1)

        qT2 = xA[:, 0:T]
        kT2 = xB[:, 0:T]
        v2 = v_area[:, :, :].rearrange("p a (t d) -> p (a t) d", d=P)
        p2 = sb("p2", [P, 2, T])
        pt2 = ffn_area[:, 0:4, :].rearrange("p a (t d) -> p (a t) d", d=P)
        st = sb("st", [P, 2, 4])
        on2 = sb("on2", [P, P])
        ot2 = sb("ot2", [P, P])
        sbank = banks[4:8]
        tbank = banks[2:4]
        A_SCALE = float(P) ** -0.5
        NQ = 2 * CHUNKS
        NV = TILES // 4

        def groups(i):
            return [(g, min(4, i + 1 - 4 * g)) for g in range(i // 4 + 1)]

        GBASE = [sum(len(groups(m)) for m in range(i)) for i in range(TILES + 1)]

        def pe_causal(pe):
            pe.wait_ge(n_x, 2 * CHUNKS + 1)
            for n in range(NQ + NV):
                if n >= 2:
                    pe.wait_ge(c_evac, n - 1 + 1)
                if n < NQ:
                    kind, j = divmod(n, CHUNKS)
                    last = nc.tensor.matmul(proj[n % 2][:, :], awqkv[:, kind * P:(kind + 1) * P],
                                            xT[:, j * BANK:(j + 1) * BANK], start=True, stop=True)
                else:
                    for m in range(4):
                        t = (n - NQ) * 4 + m
                        last = nc.tensor.matmul(proj[n % 2][:, m * P:(m + 1) * P], xT[:, t * P:(t + 1) * P],
                                                awqkv[:, 2 * P:3 * P], start=True, stop=True,
                                                skip_group_check=True)
                last.then_inc(c_proj, 1)
            pe.wait_ge(c_evac, NQ + NV + 1)

            def scores(i):
                if i >= 1:
                    pe.wait_ge(c_exp, i + 1)
                for g, m in groups(i):
                    diag = g == i // 4
                    last = nc.tensor.matmul(sbank[g][:, 0:m * P], qT2[:, i * P:(i + 1) * P],
                                            kT2[:, g * BANK:g * BANK + m * P], start=True, stop=not diag,
                                            skip_group_check=True)
                    if diag:
                        last = nc.tensor.matmul(sbank[g][:, (m - 1) * P:m * P], identb[:, :], causalb[:, :],
                                                start=False, stop=True, skip_group_check=True)
                last.then_inc(c_s, 1)

            scores(0)
            for i in range(TILES):
                pe.wait_ge(c_exp, i + 2)
                if i + 1 < TILES:
                    scores(i + 1)
                for g, m in groups(i):
                    n = GBASE[i] + g
                    if n >= 2:
                        pe.wait_ge(c_pt, n - 1 + 1)
                    for e in range(m):
                        last = nc.tensor.transpose(tbank[n % 2][:, e * P:(e + 1) * P],
                                                   p2[:, i % 2, (4 * g + e) * P:(4 * g + e + 1) * P], identf[:, :])
                    last.then_inc(c_t, 1)
                if i >= 1:
                    pe.wait_ge(c_otc, i + 1)
                for g, m in groups(i):
                    pe.wait_ge(c_pt, GBASE[i] + g + 2)
                    for e in range(m):
                        t = 4 * g + e
                        last = nc.tensor.matmul(proj[0][:, 0:P], pt2[:, t, :], v2[:, t, :],
                                                start=(t == 0), stop=(t == i))
                last.then_inc(c_o, 1)
                pe.wait_ge(c_on, i + 2)
                nc.tensor.transpose(proj[0][:, P:2 * P], on2[:, :], identf[:, :]).then_inc(c_ot, 1)
                pe.wait_ge(c_otc, i + 2)
                if i >= 1:
                    pe.wait_ge(c_x, i + 1)
                nc.tensor.matmul(proj[1][:, 0:P], awproj[:, :], ot2[:, :], start=True, stop=True)\
                    .then_inc(c_y, 1)

        def act_causal(act):
            for n in range(NQ + NV):
                act.wait_ge(c_proj, n + 2)
                if n < NQ:
                    kind, j = divmod(n, CHUNKS)
                    dst = (qT2, kT2)[kind][:, j * BANK:(j + 1) * BANK]
                else:
                    dst = v2[:, (n - NQ) * 4:(n - NQ) * 4 + 4, :].rearrange("p t d -> p (t d)")
                nc.scalar.activation(dst, proj[n % 2][:, :], ACT.Copy).then_inc(c_evac, 1)
            for i in range(TILES):
                act.wait_ge(c_neg, i + 2)
                if i >= 2:
                    act.wait_ge(c_o, i - 1 + 1)
                n = (i + 1) * P
                view = [(g, m) for g, m in groups(i)]
                for g, m in view:
                    last = nc.scalar.activation(p2[:, i % 2, g * BANK:g * BANK + m * P], sbank[g][:, 0:m * P],
                                                ACT.Exp, bias=st[:, i % 2, 1:2], scale=A_SCALE,
                                                accum_out=part[:, i % 2, g:g + 1])
                last.then_inc(c_exp, 1)

        mask32 = p2[:, 0, 0:3 * P].rearrange("p (a k) -> p a k", k=P)
        part = sb("part", [P, 2, 4])
        gmax = sb("gmax", [P, 2, 4])
        c_gmax, c_sum = sem("c_gmax"), sem("c_sum")

        def dve_causal(dve):
            def maxima(i):
                dve.wait_ge(c_s, i + 2)
                k = len(groups(i))
                for g, m in groups(i):
                    nc.vector.tensor_reduce(gmax[:, i % 2, g:g + 1], sbank[g][:, 0:m * P], AX_X, ALU.max)\
                        .then_inc(c_gmax, 1)
                dve.wait_ge(c_gmax, GBASE[i + 1] + 1)
                nc.vector.tensor_reduce(st[:, i % 2, 0:1], gmax[:, i % 2, 0:k], AX_X, ALU.max).then_inc(c_max, 1)
                dve.wait_ge(c_max, i + 2)
                nc.vector.tensor_scalar(st[:, i % 2, 1:2], st[:, i % 2, 0:1], -A_SCALE, None, ALU.mult)\
                    .then_inc(c_neg, 1)

            maxima(0)
            for i in range(TILES):
                dve.wait_ge(c_exp, i + 2)
                k = len(groups(i))
                nc.vector.tensor_reduce(st[:, i % 2, 2:3], part[:, i % 2, 0:k], AX_X, ALU.add).then_inc(c_sum, 1)
                dve.wait_ge(c_sum, i + 2)
                nc.vector.reciprocal(st[:, i % 2, 3:4], st[:, i % 2, 2:3]).then_inc(c_inv, 1)
                if i + 1 < TILES:
                    maxima(i + 1)
                for g, m in groups(i):
                    dve.wait_ge(c_t, GBASE[i] + g + 2)
                    if i >= 1:
                        dve.wait_ge(c_o, i + 1)
                    nc.vector.tensor_copy(pt2[:, 4 * g:4 * g + m, :].rearrange("p t q -> p (t q)"),
                                          tbank[(GBASE[i] + g) % 2][:, 0:m * P]).then_inc(c_pt, 1)
                dve.wait_ge(c_o, i + 2)
                dve.wait_ge(c_inv, i + 2)
                nc.vector.tensor_scalar(on2[:, :], proj[0][:, 0:P], st[:, i % 2, 3:4], None, ALU.mult)\
                    .then_inc(c_on, 1)
                dve.wait_ge(c_ot, i + 2)
                nc.vector.tensor_copy(ot2[:, :], proj[0][:, P:2 * P]).then_inc(c_otc, 1)
                dve.wait_ge(c_y, i + 2)
                s = slice(i * P, (i + 1) * P)
                nc.vector.tensor_tensor(xm[:, s], proj[1][:, 0:P], xm[:, s], ALU.add).then_inc(c_x, 1)

        LOADS = 8

        PE_SEMS = [pe_tq, pe_tk, pe_tp, pe_qk, pe_v, pe_s, pe_o, pe_y, f_mean, f_var, f_spread, f_gate, f_up,
                   f_down, n_mean, n_var, n_spread, c_proj, c_s, c_t, c_o, c_ot, c_y]
        ACT_SEMS = [act_xq, act_xv, act_qz, act_kt, act_pt, act_raw, act_sq, act_v, act_exp, act_o, f_sq, f_gelu, n_sq, c_evac,
                    c_exp]
        DVE_SEMS = [dve_ssq, dve_cos, dve_rope, dve_halo, dve_max, dve_sub, dve_sum, dve_rinv, dve_y,
                    dve_xb, dve_zero, root_done, f_root, n_root, f_xc, f_xh, f_xn, f_hid, f_x, f_shift, n_xc, n_x,
                    n_shift, h_x, c_max, c_neg, c_inv, c_pt, c_on, c_otc, c_x, c_gmax, c_sum]
        POOL_SEMS = [pool_sin, pool_qk, pool_pn, pool_tab, pool_init, pool_vz]

        def start_at_one(eng, sems):
            for s in sems:
                eng.sem_inc(s, 1)

        block = ctx.enter_context(nc.Block())

        @block.sync
        def _(sp):
            sp.dma_start(xm[:, :], x_t).then_inc(ld_const, 16)
            sp.dma_start(identf[:, :], ident).then_inc(ld_const, 16)
            sp.dma_start(mask32[:, 0:2, :], mask).then_inc(ld_const, 16)
            sp.dma_start(mask32[:, 2, :], causal).then_inc(ld_const, 16)
            sp.dma_start(reb[:, :], rebase).then_inc(ld_const, 16)
            sp.dma_start(awqkv[:, :], a_wqkv).then_inc(ld_const, 16)
            sp.dma_start(awproj[:, :], a_wproj).then_inc(ld_const, 16)
            sp.dma_start(trig_sb[:, :, :, :], trig).then_inc(ld_const, 16)
            sp.dma_start(qks[:, :, :], qk_scales[0:1, :, :].rearrange("a i d -> a (i d)")
                         .broadcast_to([P, 4 * DH]).rearrange("p (i d) -> p i d", d=DH)).then_inc(ld_scales, 16)
            sp.dma_start(wqkv[:, :], w_qkv[0, :, :]).then_inc(ld_qkv, 16)
            sp.dma_start(wo[:, :, :], w_o[0, :, :].rearrange("(j r) c -> r j c", r=P)).then_inc(ld_o, 16)
            for blk in range(2):
                with sp.Fori(0, DEPTH) as l:
                    sp_layer(sp, l + blk * DEPTH, l)
            sp.wait_ge(ld_scales, (2 * DEPTH + 1) * 16)
            sp.wait_ge(ld_qkv, (2 * DEPTH + 1) * 16)
            sp.wait_ge(ld_o, (2 * DEPTH + 1) * 16)
            for j in range(CHUNKS):
                sp.wait_ge(h_x, CHUNKS + j + 2)
                sp.dma_start(out_t[:, j * BANK:(j + 1) * BANK], xm[:, j * BANK:(j + 1) * BANK]).then_inc(out_done, 16)
            sp.wait_ge(out_done, CHUNKS * 16)

        @block.gpsimd
        def _(pool):
            start_at_one(pool, POOL_SEMS)
            nc.gpsimd.memset(mean_w[:, :], 1.0 / P)
            nc.gpsimd.memset(qz[:, :, :, :, :], 0.0).then_inc(pool_init, 1)
            pool.wait_ge(ld_const, LOADS * 16)
            fold_scales(pool, 0)
            for blk in range(2):
                pool.wait_ge(n_shift, (blk + 1) * CHUNKS + 1)
                with pool.Fori(0, DEPTH) as l:
                    pool_attention(pool, l + blk * DEPTH)
                    pool_ffn(pool, l + blk * DEPTH)

        @block.scalar
        def _(act):
            start_at_one(act, ACT_SEMS)
            act_norm(act, 0)
            act.wait_ge(pool_init, 1 + 1)
            for blk in range(2):
                act.wait_ge(n_shift, (blk + 1) * CHUNKS + 1)
                with act.Fori(0, DEPTH) as l:
                    act_attention(act, l + blk * DEPTH)
                    act_ffn(act, l + blk * DEPTH)
                if blk == 0:
                    act_norm(act, 1)
                    act_causal(act)
                    act_norm(act, 2)

        @block.vector
        def _(dve):
            start_at_one(dve, DVE_SEMS)
            def no_token_before():
                nc.vector.memset(xA[64:P, 0:1], 0.0)
                nc.vector.memset(xB[64:P, 0:1], 0.0).then_inc(dve_zero, 1)

            no_token_before()
            dve.wait_ge(ld_const, LOADS * 16)
            nc.vector.tensor_copy(identb[:, :], identf[:, :])
            nc.vector.tensor_copy(causalb[:, :], mask32[:, 2, :])
            nc.vector.tensor_copy(maskb[:, :, :], mask32[:, 0:2, :]).then_inc(dve_masks, 1)
            dve_norm(dve, 0)
            for blk in range(2):
                with dve.Fori(0, DEPTH) as l:
                    dve_attention(dve, l + blk * DEPTH)
                    dve_ffn(dve, l + blk * DEPTH)
                dve_half_step(dve, blk)
                if blk == 0:
                    dve_norm(dve, 1)
                    dve_causal(dve)
                    no_token_before()
                    dve_norm(dve, 2)

        @block.tensor
        def _(pe):
            start_at_one(pe, PE_SEMS)
            pe_norm(pe, 0)
            pe.wait_ge(dve_masks, 1)
            for blk in range(2):
                with pe.Fori(0, DEPTH) as l:
                    pe_attention(pe, l + blk * DEPTH)
                    pe_ffn(pe, l + blk * DEPTH)
                if blk == 0:
                    pe_norm(pe, 1)
                    pe_causal(pe)
                    pe_norm(pe, 2)


def _constants(T):
    import numpy as np
    half = np.arange(0, DH, 2, dtype=np.float32)
    inv_freq = (np.float32(1.0) / np.power(np.float32(10000.0), half / np.float32(DH))).astype(np.float32)
    t = np.arange(T, dtype=np.float32)
    ang = (t[:, None] * inv_freq[None, :]).astype(np.float32).astype(np.float64)
    ang = np.concatenate([ang, ang], -1)
    base = ((half + 0.4 * DH) / (1.4 * DH)).astype(np.float32).astype(np.float64)
    base = np.concatenate([base, base])
    power = (np.arange(T) % TILE - TILE // 2) / (WINDOW // 2)
    scale = base[None, :] ** power[:, None]
    sign = np.where(np.arange(DH) < DH // 2, -1.0, 1.0)[None, :]
    tabs = np.stack([np.cos(ang) * scale, sign * np.sin(ang) * scale, np.cos(ang) / scale, sign * np.sin(ang) / scale])
    trig = tabs.reshape(4, T // TILE, TILE, DH).transpose(2, 0, 1, 3).astype(np.float32)
    rebase = np.tile(base ** (TILE / (WINDOW // 2)), 2)[:, None].astype(np.float32)
    q = np.arange(P) % WINDOW
    wl = np.arange(P) // 64
    j = np.arange(P) % 64
    u = np.arange(P) // 64
    band = (j[None, :] >= q[:, None]) & (j[None, :] <= q[:, None] + WINDOW)
    start = band & ~((wl[:, None] == 0) & (u[None, :] == 0) & (j[None, :] < WINDOW))
    mask = np.where(np.stack([start, band], 1), 0.0, -1e30).astype(np.float32)
    ident = np.eye(P, dtype=np.float32)
    causal = np.where(np.arange(P)[:, None] >= np.arange(P)[None, :], 0.0, -1e30).astype(np.float32)
    return trig, rebase, mask, ident, causal


def kernel(**inputs):
    import numpy as np
    import concourse.bacc as bacc
    from concourse import mybir as mb
    from concourse.bass_utils import run_bass_kernel_spmd as run

    g = {k: np.asarray(v) for k, v in inputs.items()}
    x = g["L0_attn_x"]
    T = x.shape[1]
    trig, rebase, mask, ident, causal = _constants(T)

    def again(a):
        return np.concatenate([a, a[:1]], 0)

    def swap(a):
        return np.concatenate([a[:, DH // 2:], a[:, :DH // 2]], 1)

    qs, ks = g["L0_ffn_q_scale"], g["L0_ffn_k_scale"]
    scales = again(np.stack([qs, swap(qs), ks, swap(ks)], 1))
    vecs = np.zeros((DEPTH, P, 9), np.float32)
    for i, name in enumerate(("L0_ffn_ln_g", "L0_ffn_ln_b", "L0_ffn_b2")):
        vecs[:, :, i] = g[name]
    b1 = g["L0_ffn_b1"]
    for k, (off, n) in enumerate(HCH):
        vecs[:, :n, 3 + k] = b1[:, off:off + n]
        vecs[:, :n, 6 + k] = b1[:, HIDDEN + off:HIDDEN + off + n]
    arrays = {
        "x_t": x[0].T, "w_qkv": again(g["L0_ffn_Wqkv"]), "w_o": again(g["L0_ffn_Wo"]),
        "w_1": g["L0_ffn_W1"], "w_2": g["L0_ffn_W2"], "vecs": vecs, "qk_scales": scales, "trig": trig,
        "rebase": rebase, "mask": mask, "ident": ident, "causal": causal,
        "a_wqkv": g["L0_attn_Wqkv"], "a_wproj": g["L0_attn_Wproj"],
    }
    arrays = {k: np.ascontiguousarray(v) for k, v in arrays.items()}
    nc = bacc.Bacc("TRN2", target_bir_lowering=False, num_devices=1)
    ap = {k: nc.dram_tensor(k + "_dram", v.shape, mb.dt.from_np(v.dtype), kind="ExternalInput").ap() for k, v in arrays.items()}
    out = nc.dram_tensor("out_t_dram", (P, T), mb.dt.float32, kind="ExternalOutput").ap()
    bass_macaron(nc, ap["x_t"], ap["w_qkv"], ap["w_o"], ap["w_1"], ap["w_2"], ap["vecs"], ap["qk_scales"],
                 ap["trig"], ap["rebase"], ap["mask"], ap["ident"], ap["causal"],
                 ap["a_wqkv"], ap["a_wproj"], out)
    r = run(nc, [{k + "_dram": v for k, v in arrays.items()}], core_ids=[0])
    return np.ascontiguousarray(r.results[0]["out_t_dram"].T)[None]
```

```python
from contextlib import ExitStack

import concourse.bass as bass
from concourse import mybir

F32 = mybir.dt.float32
BF16 = mybir.dt.bfloat16
I32 = mybir.dt.int32
ALU = mybir.AluOpType
ACT = mybir.ActivationFunctionType
AX_X = mybir.AxisListType.X

P = 128
TILE = 128
WINDOW = 32
DH = 64
PAIRS = 8
HALVES = 2
PPH = PAIRS // HALVES
HEADS_PER_HALF = 2 * PPH
HEADS = 2 * PAIRS
ROOTS = 2 * HEADS + 1
BANK = 512
DEPTH = 6
HIDDEN = 341
HCH = [(0, 128), (128, 128), (256, HIDDEN - 256)]
QK_SCALE = 8.0
EPS = 1e-5
ROOT_STEPS = 10


def bass_macaron(nc, x_t, w_qkv, w_o, w_1, w_2, vecs, qk_scales, trig, rebase, mask, ident, causal,
                 a_wqkv, a_wproj, out_t):
    T = x_t.shape[1]
    TILES = T // TILE
    CHUNKS = T // BANK

    ctx = ExitStack()
    with ctx:
        def sb(name, shape, dt=F32):
            return ctx.enter_context(nc.sbuf_tensor(name, shape, dt))

        def sem(name):
            return ctx.enter_context(nc.semaphore(name))

        banks = [ctx.enter_context(nc.psum_tensor(f"bank{i}", [P, BANK], F32)) for i in range(8)]
        proj = banks[0:2]
        tran = banks[2:4]
        score = banks[4:6]
        outp = banks[6:8]

        wqkv = sb("wqkv", [P, 3 * PAIRS * P])
        wo = sb("wo", [P, PAIRS, P])
        w1 = sb("w1", [P, 2 * HIDDEN])
        w2 = sb("w2", [P, 3, P])
        vec = sb("vec", [P, 9])
        scales = sb("scales", [P, DEPTH, 4, DH])
        trig_sb = sb("trig_sb", [P, 4, TILES, DH])
        tab = sb("tab", [P, 4, DH])
        reb = sb("reb", [P, 1])
        maskb = sb("maskb", [P, 2, P], BF16)
        identb = sb("identb", [P, P], BF16)
        identf = sb("identf", [P, P])
        causalb = sb("causalb", [P, P], BF16)
        mean_w = sb("mean_w", [P, P])
        awqkv = sb("awqkv", [P, 3 * P])
        awproj = sb("awproj", [P, P])

        xm = sb("xm", [P, T])
        xT = sb("xT", [P, T])
        xA = sb("xA", [P, T + 1])
        xB = sb("xB", [P, T + 1])

        xq = sb("xq", [P, TILE])
        xv = sb("xv", [P, TILE])
        raw = sb("raw", [P, 2 * HALVES, BANK])
        sq = sb("sq", [P, HALVES, BANK])
        sums = sb("sums", [P, ROOTS])
        ssq = sums[:, 0:2 * HEADS].rearrange("p (e h) -> p e h", h=HEADS_PER_HALF)
        inv = sb("inv", [P, ROOTS])
        rnorm = inv[:, 0:2 * HEADS].rearrange("p (e h) -> p e h", h=HEADS_PER_HALF)
        root_s = sb("root_s", [P, ROOTS])
        root_t = sb("root_t", [P, ROOTS])
        root_u = sb("root_u", [P, ROOTS])
        sinp = sb("sinp", [P, 2 * HALVES, BANK])
        qk = sb("qk", [P, 2 * HALVES, BANK])
        qz = sb("qz", [P, PAIRS, 4, 2, WINDOW])
        kT = sb("kT", [P, PAIRS, WINDOW + TILE])
        pb = sb("pb", [P, HALVES, BANK])
        mx = sb("mx", [P, HALVES, HEADS_PER_HALF])
        sm = sb("sm", [P, HALVES, HEADS_PER_HALF])
        rinv = sb("rinv", [P, HALVES, HEADS_PER_HALF])
        pT = sb("pT", [P, PAIRS, 2, 2, 2, WINDOW])
        v_area = sb("v_area", [P, 2 * HALVES, BANK])
        vt = v_area[:, 0:HALVES, :]
        vs = v_area[:, HALVES:, :]
        oT = sb("oT", [P, PAIRS, TILE])

        fxc = sb("fxc", [P, TILE])
        fxsq = sb("fxsq", [P, TILE])
        fxh = sb("fxh", [P, TILE])
        fxn = sb("fxn", [P, TILE])
        gate = sb("gate", [P, 3, TILE])
        hid = sb("hid", [P, 3, TILE])

        rstd = sb("rstd", [P, TILES])

        ld_const = sem("ld_const")
        ld_q, ld_k, ld_v, ld_o, ld_ffn = (sem(s) for s in ("ld_q", "ld_k", "ld_v", "ld_o", "ld_ffn"))
        pe_tq, pe_tk, pe_tp = sem("pe_tq"), sem("pe_tk"), sem("pe_tp")
        pe_qk, pe_v, pe_s, pe_o, pe_y = (sem(s) for s in ("pe_qk", "pe_v", "pe_s", "pe_o", "pe_y"))
        act_qz, act_kt, act_pt = sem("act_qz"), sem("act_kt"), sem("act_pt")
        act_raw, act_sq, act_v, act_exp, act_o = (sem(s) for s in ("act_raw", "act_sq", "act_v", "act_exp", "act_o"))
        act_xq, act_xv = sem("act_xq"), sem("act_xv")
        dve_ssq, dve_cos, dve_rope, dve_halo = (sem(s) for s in ("dve_ssq", "dve_cos", "dve_rope", "dve_halo"))
        dve_max, dve_sub, dve_sum, dve_rinv, dve_y = (
            sem(s) for s in ("dve_max", "dve_sub", "dve_sum", "dve_rinv", "dve_y"))
        pool_sin, pool_qk, pool_pn, dve_xb = (sem(s) for s in ("pool_sin", "pool_qk", "pool_pn", "dve_xb"))
        pool_tab, pool_init, dve_vz = sem("pool_tab"), sem("pool_init"), sem("dve_vz")
        pool_held, pe_held, dve_zero, dve_masks = sem("pool_held"), sem("pe_held"), sem("dve_zero"), sem("dve_masks")
        root_done, f_root, n_root = sem("root_done"), sem("f_root"), sem("n_root")
        v_moved = [sem(f"v_moved{h}") for h in range(HALVES)]
        v_carried = sem("v_carried")
        f_mean, f_xc, f_sq, f_var, f_eps, f_spread, f_xh, f_xn = (
            sem(s) for s in ("f_mean", "f_xc", "f_sq", "f_var", "f_eps", "f_spread", "f_xh", "f_xn"))
        f_gate, f_up, f_gelu, f_hid, f_down, f_x, f_shift = (
            sem(s) for s in ("f_gate", "f_up", "f_gelu", "f_hid", "f_down", "f_x", "f_shift"))
        n_mean, n_xc, n_sq, n_var, n_spread, n_x, n_shift = (
            sem(s) for s in ("n_mean", "n_xc", "n_sq", "n_var", "n_spread", "n_x", "n_shift"))
        h_x = sem("h_x")
        c_proj, c_evac, c_s, c_max, c_neg, c_exp, c_inv, c_t, c_pt, c_o, c_on, c_ot, c_x = (
            sem(s) for s in ("c_proj", "c_evac", "c_s", "c_max", "c_neg", "c_exp", "c_inv", "c_t", "c_pt",
                             "c_o", "c_on", "c_ot", "c_x"))
        out_done = sem("out_done")

        def heads(ap):
            return ap.rearrange("p (h d) -> p h d", d=DH)

        def per_head(ap):
            return ap.unsqueeze(2).broadcast_to([P, HEADS_PER_HALF, DH])

        def over_heads(ap, n=DH):
            return ap.unsqueeze(1).broadcast_to([P, HEADS_PER_HALF, n])

        class At:
            def __init__(self, blk, l, t):
                self.t, self.l, self.L = t, l, l + blk * DEPTH
                self.n = self.L * TILES + t
                self.first = isinstance(t, int) and t == 0
                self.t_late = False

        STAGES = 6

        def block_steps(eng, blk, step, apart=False):
            last = TILES - 1 if apart else TILES

            def own(l, s):
                return [At(blk, l, s - k) if not isinstance(s, int) or 0 <= s - k < TILES else None
                        for k in range(STAGES)]

            def layer_begins(l, s):
                return [At(blk, l, s - k) if s >= k else At(blk, l - 1, TILES + s - k) for k in range(STAGES)]

            for s in range(STAGES):
                step(s, *own(0, s))
            with eng.Fori(STAGES, last) as s:
                step(s, *own(0, s))
            if apart:
                step(TILES - 1, *own(0, TILES - 1))
            with eng.Fori(1, DEPTH) as l:
                for s in range(STAGES):
                    step(s, *layer_begins(l, s))
                with eng.Fori(STAGES, last) as s:
                    step(s, *own(l, s))
                if apart:
                    step(TILES - 1, *own(l, TILES - 1))
            for s in range(TILES, TILES + STAGES - 1):
                tiles = own(DEPTH - 1, s)
                for at in tiles:
                    if at is not None:
                        at.t_late = at.t > TILES - STAGES + 1
                step(s, *tiles)

        def late_root(e, blk):
            return blk * (STAGES - 2) + e.t - (TILES - STAGES + 2)

        def tile_of(buf, t):
            return buf[:, t * TILE:(t + 1) * TILE] if isinstance(t, int) else buf[:, bass.ds(t * TILE, TILE)]

        def pe_block(pe, blk):
            def p_times_v(d, part):
                h, second = divmod(part, 2)
                if not second:
                    pe.wait_ge(act_pt, d.n * 2 + (h + 1) + 1)
                    pe.wait_ge(act_v, d.n * 2 + (h + 1) + 1)
                    pe.wait_ge(v_moved[h], (d.n + 1) * 16)
                    if d.first:
                        pe.wait_ge(dve_vz, d.L + 2)
                    else:
                        pe.wait_ge(v_carried, (d.L * (TILES - 1) + d.t) * 16)
                    pe.sem_inc(pe_held, 1)
                for j in (2 * second, 2 * second + 1):
                    for wl in range(2):
                        src = vt if wl else vs
                        for i in range(2):
                            pr = h * PPH + j
                            last = nc.tensor.matmul(
                                outp[wl][64 * i:64 * i + 64, pr * 64:(pr + 1) * 64],
                                src[:, h, j * P + i * DH:j * P + (i + 1) * DH],
                                pT[:, pr, wl, i, :, :].rearrange("p u q -> p (u q)"),
                                start=True, stop=True, skip_group_check=True)
                if second:
                    last.then_inc(pe_o, 1)

            def step(s, a, b, c, d, e, f):
                if b is not None:
                    for h in range(HALVES):
                        pe.wait_ge(pool_qk, b.n * 4 + (h + 1) + 1)
                        pe.wait_ge(act_kt, b.n * 2 + 1)
                        if d is not None:
                            pe.wait_ge(act_pt, d.n * 2 + 2 + 1)
                        for j in range(PPH):
                            last = nc.tensor.transpose(tran[h][:, j * P:(j + 1) * P],
                                                       qk[:, h, j * P:(j + 1) * P], identf[:, :])
                        last.then_inc(pe_tq, 1)
                if a is not None:
                    if a.first:
                        pe.wait_ge(ld_q, (a.L + 1) * 16)
                        pe.wait_ge(ld_k, (a.L + 1) * 16)
                    pe.wait_ge(act_xq, a.n + 2)
                    pe.wait_ge(act_sq, a.n * 4 + 1)
                    if d is not None:
                        pe.wait_ge(act_v, d.n * 2 + 2 + 1)
                    for h in range(HALVES):
                        nc.tensor.matmul(proj[h][:, :], xq[:, :], wqkv[:, h * BANK:(h + 1) * BANK],
                                         start=True, stop=True).then_inc(pe_qk, 1)
                if b is not None:
                    for h in range(HALVES):
                        pe.wait_ge(pool_qk, b.n * 4 + (h + 3) + 1)
                        pe.wait_ge(act_qz, b.n * 2 + (h + 1) + 1)
                        for j in range(PPH):
                            last = nc.tensor.transpose(tran[h][:, j * P:(j + 1) * P],
                                                       qk[:, 2 + h, j * P:(j + 1) * P], identf[:, :])
                        last.then_inc(pe_tk, 1)
                if d is not None:
                    pe.wait_ge(act_o, d.n * 2 + 1)
                    pe.wait_ge(dve_y, d.n + 1)
                for part in range(4):
                    if d is not None:
                        p_times_v(d, part)
                    h = part % 2
                    if part < 2 and a is not None:
                        pe.wait_ge(act_sq, a.n * 4 + (h + 1) + 1)
                        nc.tensor.matmul(proj[h][:, :], xq[:, :],
                                         wqkv[:, PAIRS * P + h * BANK:PAIRS * P + (h + 1) * BANK],
                                         start=True, stop=True).then_inc(pe_qk, 1)
                    if part == 0 and c is not None:
                        pe.wait_ge(dve_sub, c.n * 2 + 2 + 1)
                    if part == 0 and f is not None:
                        if f.t_late:
                            pe.wait_ge(f_root, (late_root(f, blk) + 1) * ROOT_STEPS + 1)
                        else:
                            pe.wait_ge(root_done, (f.n + 5) * ROOT_STEPS + 1)
                        nc.tensor.matmul(score[1][:, 0:TILE], inv[:, ROOTS - 1:ROOTS].broadcast_to([P, P]),
                                         identf[:, :], start=True, stop=True).then_inc(f_spread, 1)
                    if part == 0 and e is not None:
                        pe.wait_ge(dve_xb, e.n + 2)
                        nc.tensor.matmul(score[0][:, 0:TILE], mean_w[:, :], tile_of(xB, e.t),
                                         start=True, stop=True).then_inc(f_mean, 1)
                    if part == 1 and f is not None:
                        if f.first:
                            pe.wait_ge(ld_ffn, (f.L + 1) * 64)
                        pe.wait_ge(f_xn, f.n + 2)
                        if e is not None:
                            pe.wait_ge(f_xc, e.n + 2)
                        for k, (off, n) in enumerate(HCH):
                            last = nc.tensor.matmul(score[0][0:n, k * TILE:(k + 1) * TILE],
                                                    w1[:, HIDDEN + off:HIDDEN + off + n], fxn[:, :],
                                                    start=True, stop=True, skip_group_check=True)
                        last.then_inc(f_gate, 1)
                    if part == 2 and f is not None:
                        for k, (off, n) in enumerate(HCH):
                            last = nc.tensor.matmul(score[1][0:n, k * TILE:(k + 1) * TILE],
                                                    w1[:, off:off + n], fxn[:, :],
                                                    start=True, stop=True, skip_group_check=True)
                        last.then_inc(f_up, 1)
                    if part >= 2 and c is not None:
                        if c.first and part == 2:
                            pe.wait_ge(ld_v, (c.L + 1) * 16)
                        pe.wait_ge(act_xv, c.n + 2)
                        if a is not None:
                            pe.wait_ge(act_sq, a.n * 4 + (h + 3) + 1)
                        else:
                            pe.wait_ge(act_v, c.n * 2 + 1)
                        nc.tensor.matmul(proj[h][:, :], xv[:, :],
                                         wqkv[:, 2 * PAIRS * P + h * BANK:2 * PAIRS * P + (h + 1) * BANK],
                                         start=True, stop=True).then_inc(pe_v, 1)
                    if part == 2 and e is not None:
                        pe.wait_ge(f_sq, e.n + 2)
                        pe.wait_ge(f_eps, e.n + 1)
                        if b is not None:
                            pe.wait_ge(act_kt, b.n * 2 + 2 + 1)
                        elif d is not None:
                            pe.wait_ge(act_pt, d.n * 2 + 2 + 1)
                        nc.tensor.matmul(tran[1][:, 0:1], fxsq[:, :], mean_w[:, 0:1], start=True, stop=True)\
                            .then_inc(f_var, 1)
                if f is not None:
                    pe.wait_ge(f_hid, f.n + 2)
                    pe.wait_ge(f_x, f.n + 1)
                    if b is not None:
                        pe.wait_ge(act_kt, b.n * 2 + 1 + 1)
                    elif d is not None:
                        pe.wait_ge(act_pt, d.n * 2 + 1 + 1)
                    for k, (off, n) in enumerate(HCH):
                        last = nc.tensor.matmul(tran[0][:, 0:TILE], w2[0:n, k, :], hid[0:n, k, :],
                                                start=(k == 0), stop=(k == 2))
                    last.then_inc(f_down, 1)
                if b is not None:
                    first = 0 if b.first else 1
                    pe.wait_ge(dve_halo, b.n + 2)
                    pe.wait_ge(dve_sub, b.n * 2 + 1)
                    for h in range(HALVES):
                        pe.wait_ge(act_kt, b.n * 2 + (h + 1) + 1)
                        nc.tensor.matmul(score[h][:, :].rearrange("p (j k) -> p j k", k=P), identb[:, :],
                                         maskb[:, first, :].unsqueeze(1).broadcast_to([P, PPH, P]),
                                         start=True, stop=False, skip_group_check=True)
                        for j in range(PPH):
                            for w in range(4):
                                u, wl = divmod(w, 2)
                                pr = h * PPH + j
                                last = nc.tensor.matmul(
                                    score[h][64 * wl:64 * wl + 64, j * P + u * 64:j * P + u * 64 + 64],
                                    qz[:, pr, w, :, :].rearrange("p a q -> p (a q)"),
                                    kT[:, pr, WINDOW * w:WINDOW * w + 64],
                                    start=False, stop=(j == PPH - 1 and w == 3), skip_group_check=True)
                        last.then_inc(pe_s, 1)
                if c is not None:
                    if f is not None:
                        pe.wait_ge(f_x, f.n + 2)
                    if e is not None:
                        pe.wait_ge(f_eps, e.n + 2)
                    for h in range(HALVES):
                        pe.wait_ge(pool_pn, c.n * 2 + (h + 1) + 1)
                        if b is not None:
                            pe.wait_ge(act_kt, b.n * 2 + (h + 1) + 1)
                        else:
                            pe.wait_ge(act_pt, c.n * 2 + 1)
                        for j in range(PPH):
                            last = nc.tensor.transpose(tran[h][:, j * P:(j + 1) * P],
                                                       pb[:, h, j * P:(j + 1) * P], identf[:, :])
                        last.then_inc(pe_tp, 1)
                if d is not None:
                    if d.first:
                        pe.wait_ge(ld_o, (d.L + 1) * 16)
                    pe.wait_ge(act_o, d.n * 2 + 2 + 1)
                    for pr in range(PAIRS):
                        last = nc.tensor.matmul(outp[0][:, 0:TILE], wo[:, pr, :], oT[:, pr, :],
                                                start=(pr == 0), stop=(pr == PAIRS - 1))
                    last.then_inc(pe_y, 1)
            block_steps(pe, blk, step)

        def act_block(act, blk):
            def step(s, a, b, c, d, e, f):
                def parts(*which):
                    for i in which:
                        act.wait_ge(pe_qk, a.n * 4 + (i + 1) + 1)
                        act.wait_ge(pool_sin, a.n * 4 + 1)
                        act.wait_ge(dve_cos, a.n * 4 + 1)
                        nc.scalar.activation(raw[:, i, :], proj[i % 2][:, :], ACT.Copy).then_inc(act_raw, 1)
                        act.wait_ge(dve_ssq, a.n * 4 + max(0, i - 1) + 1)
                        nc.scalar.activation(sq[:, i % 2, :], proj[i % 2][:, :], ACT.Square).then_inc(act_sq, 1)

                if a is not None:
                    act.wait_ge(pe_qk, a.n * 4 + 1)
                    if not isinstance(a.L, int):
                        act.wait_ge(f_shift, a.n - TILES + 2)
                    nc.scalar.activation(xq[:, :], tile_of(xA, a.t), ACT.Copy).then_inc(act_xq, 1)
                if c is not None:
                    act.wait_ge(pe_v, c.n * 2 + 1)
                    nc.scalar.activation(xv[:, :], tile_of(xA, c.t), ACT.Copy).then_inc(act_xv, 1)
                if b is not None:
                    for h in range(HALVES):
                        act.wait_ge(pe_tq, b.n * 2 + (h + 1) + 1)
                        act.wait_ge(pe_s, b.n * 2 + 1)
                        for i in range(2):
                            last = nc.scalar.activation(
                                qz[64 * i:64 * i + 64, h * PPH:(h + 1) * PPH, :, i, :],
                                tran[h][64 * i:64 * i + 64, :].rearrange("p (j w q) -> p j w q", w=4, q=WINDOW),
                                ACT.Copy)
                        last.then_inc(act_qz, 1)
                if a is not None:
                    parts(0, 1)
                if b is not None:
                    act.wait_ge(dve_halo, b.n + 2)
                    for h in range(HALVES):
                        act.wait_ge(pe_tk, b.n * 2 + (h + 1) + 1)
                        nc.scalar.activation(kT[:, h * PPH:(h + 1) * PPH, WINDOW:],
                                             tran[h][:, :].rearrange("p (j t) -> p j t", t=TILE),
                                             ACT.Copy).then_inc(act_kt, 1)
                if c is not None:
                    for h in range(HALVES):
                        act.wait_ge(dve_sub, c.n * 2 + (h + 1) + 1)
                        nc.scalar.activation(pb[:, h, :], pb[:, h, :], ACT.Exp, scale=QK_SCALE)\
                            .then_inc(act_exp, 1)
                if e is not None:
                    act.wait_ge(f_xc, e.n + 2)
                    act.wait_ge(f_var, e.n + 1)
                    nc.scalar.activation(fxsq[:, :], fxc[:, :], ACT.Square).then_inc(f_sq, 1)
                if a is not None:
                    parts(2, 3)
                if f is not None:
                    if f.first:
                        act.wait_ge(ld_ffn, (f.L + 1) * 64)
                    act.wait_ge(f_gate, f.n + 2)
                    act.wait_ge(f_hid, f.n + 1)
                    for k, (off, n) in enumerate(HCH):
                        last = nc.scalar.activation(gate[0:n, k, :], score[0][0:n, k * TILE:(k + 1) * TILE],
                                                    ACT.Gelu, bias=vec[0:n, 6 + k:7 + k])
                    last.then_inc(f_gelu, 1)
                if d is not None:
                    act.wait_ge(pe_y, d.n + 1)
                    act.wait_ge(pe_o, d.n * 2 + 2 + 1)
                    for wl in range(2):
                        nc.scalar.activation(
                            oT[:, :, :].rearrange("p j (u w q) -> p j u w q", u=2, w=2)[:, :, :, wl, :],
                            outp[wl][:, :].rearrange("p (j u q) -> p j u q", u=2, q=WINDOW), ACT.Copy)\
                            .then_inc(act_o, 1)
                if c is not None:
                    act.wait_ge(pe_o, c.n * 2 + 1)
                    if not c.first:
                        act.wait_ge(v_carried, (c.L * (TILES - 1) + c.t) * 16)
                    for h in range(HALVES):
                        act.wait_ge(pe_v, c.n * 2 + (h + 1) + 1)
                        nc.scalar.activation(vt[:, h, :], proj[h][:, :], ACT.Copy).then_inc(act_v, 1)
                    for h in range(HALVES):
                        act.wait_ge(pe_tp, c.n * 2 + (h + 1) + 1)
                        for u in range(2):
                            last = nc.scalar.activation(
                                pT[64 * u:64 * u + 64, h * PPH:(h + 1) * PPH, :, :, u, :],
                                tran[h][64 * u:64 * u + 64, :].rearrange("p (j w i q) -> p j w i q",
                                                                         w=2, i=2, q=WINDOW),
                                ACT.Copy)
                        last.then_inc(act_pt, 1)
            act.wait_ge(n_shift, (blk + 1) * CHUNKS + 1)
            block_steps(act, blk, step)

        def shift(dst, src, start, n):
            if isinstance(start, int):
                now, later = slice(start, start + n), slice(start + 1, start + 1 + n)
            else:
                now, later = bass.ds(start, n), bass.ds(start + 1, n)
            nc.vector.tensor_copy(dst[0:64, now], src[0:64, now])
            return nc.vector.tensor_copy(dst[64:P, later], src[64:P, now])

        def inverse_root(dve, src, floor, floor_op, y, done, base):
            w = src.shape[1]
            r_, t_, u_ = root_s[:, 0:w], root_t[:, 0:w], root_u[:, 0:w]
            nc.vector.tensor_scalar(r_, src, floor, 64.0 / 9.0, floor_op, ALU.mult).then_inc(done, 1)
            dve.wait_ge(done, base + 1)
            nc.vector.tensor_scalar(t_.bitcast(I32), r_.bitcast(I32), 1, None, ALU.arith_shift_right)\
                .then_inc(done, 1)
            dve.wait_ge(done, base + 2)
            nc.vector.tensor_scalar(y.bitcast(I32), t_.bitcast(I32), -1.0, float(0x5f3759df), ALU.mult, ALU.add)\
                .then_inc(done, 1)
            dve.wait_ge(done, base + 3)
            nc.vector.tensor_tensor(t_, y, y, ALU.mult).then_inc(done, 1)
            dve.wait_ge(done, base + 4)
            nc.vector.tensor_tensor(t_, t_, r_, ALU.mult).then_inc(done, 1)
            dve.wait_ge(done, base + 5)
            nc.vector.scalar_tensor_tensor(u_, t_, -10.0 / 3.0, t_, ALU.add, ALU.mult).then_inc(done, 1)
            dve.wait_ge(done, base + 6)
            nc.vector.scalar_tensor_tensor(y, u_, 5.0, y, ALU.add, ALU.mult).then_inc(done, 1)
            dve.wait_ge(done, base + 7)
            nc.vector.tensor_tensor(t_, y, y, ALU.mult).then_inc(done, 1)
            dve.wait_ge(done, base + 8)
            nc.vector.scalar_tensor_tensor(t_, t_, -0.5 * 9.0 / 64.0, r_, ALU.mult, ALU.mult).then_inc(done, 1)
            dve.wait_ge(done, base + 9)
            nc.vector.scalar_tensor_tensor(y, t_, 1.5, y, ALU.add, ALU.mult).then_inc(done, 1)

        def dve_block(dve, blk):
            def cosine_and_sums(a, i):
                if i == 0:
                    dve.wait_ge(pool_tab, a.n + 2)
                dve.wait_ge(act_raw, a.n * 4 + (i + 1) + 1)
                dve.wait_ge((pe_tq, pe_tk)[i // 2], a.n * 2 + 1)
                nc.vector.tensor_tensor(heads(qk[:, i, :]), heads(raw[:, i, :]), over_heads(tab[:, i // 2 * 2, :]),
                                        ALU.mult).then_inc(dve_cos, 1)
                dve.wait_ge(act_sq, a.n * 4 + (i + 1) + 1)
                nc.vector.tensor_reduce(ssq[:, i, :], heads(sq[:, i % 2, :]), AX_X, ALU.add).then_inc(dve_ssq, 1)

            def rotate(a, i):
                dve.wait_ge(pool_sin, a.n * 4 + (i + 1) + 1)
                dve.wait_ge(dve_cos, a.n * 4 + (i + 1) + 1)
                nc.vector.tensor_tensor(qk[:, i, :], qk[:, i, :], sinp[:, i, :], ALU.add).then_inc(dve_rope, 1)

            def step(s, a, b, c, d, e, f):
                if c is not None:
                    for h in range(HALVES):
                        dve.wait_ge(pe_s, c.n * 2 + (h + 1) + 1)
                        dve.wait_ge(dve_sub, c.n * 2 + 1)
                        nc.vector.tensor_reduce(mx[:, h, :], heads(score[h][:, :]), AX_X, ALU.max)\
                            .then_inc(dve_max, 1)
                        dve.wait_ge(dve_max, c.n * 2 + (h + 1) + 1)
                        dve.wait_ge(pe_tp, c.n * 2 + 1)
                        nc.vector.tensor_tensor(heads(pb[:, h, :]), heads(score[h][:, :]), per_head(mx[:, h, :]),
                                                ALU.subtract).then_inc(dve_sub, 1)
                if e is not None:
                    dve.wait_ge(pe_y, e.n + 2)
                    xt = tile_of(xT, e.t)
                    nc.vector.tensor_tensor(xt, outp[0][:, 0:TILE], xt, ALU.add).then_inc(dve_y, 1)
                    dve.wait_ge(dve_y, e.n + 2)
                    shift(xB, xT, e.t * TILE, TILE).then_inc(dve_xb, 1)
                if b is not None:
                    dve.wait_ge(pe_s, b.n * 2 + 1)
                    if b.first:
                        nc.vector.memset(kT[:, :, 0:WINDOW], 0.0).then_inc(dve_halo, 1)
                    else:
                        dve.wait_ge(act_kt, b.n * 2 + 1)
                        nc.vector.tensor_scalar(kT[:, :, 0:WINDOW], kT[:, :, TILE:TILE + WINDOW], reb[:, 0:1], None,
                                                ALU.mult).then_inc(dve_halo, 1)
                if a is not None:
                    cosine_and_sums(a, 0)
                    cosine_and_sums(a, 1)
                if f is not None:
                    if f.first:
                        dve.wait_ge(ld_ffn, (f.L + 1) * 64)
                    dve.wait_ge(f_spread, f.n + 2)
                    nc.vector.tensor_tensor(fxh[:, :], fxc[:, :], score[1][:, 0:TILE], ALU.mult).then_inc(f_xh, 1)
                    dve.wait_ge(f_xh, f.n + 2)
                    dve.wait_ge(f_up, f.n + 1)
                    nc.vector.tensor_scalar(fxn[:, :], fxh[:, :], vec[:, 0:1], vec[:, 1:2], ALU.mult, ALU.add)\
                        .then_inc(f_xn, 1)
                if e is not None:
                    dve.wait_ge(f_mean, e.n + 2)
                    dve.wait_ge(f_xh, e.n + 1)
                    dve.wait_ge(f_sq, e.n + 1)
                    nc.vector.tensor_tensor(fxc[:, :], tile_of(xB, e.t), score[0][:, 0:TILE], ALU.subtract)\
                        .then_inc(f_xc, 1)
                if a is not None:
                    rotate(a, 0)
                    rotate(a, 1)
                if c is not None:
                    for h in range(HALVES):
                        dve.wait_ge(act_exp, c.n * 2 + (h + 1) + 1)
                        dve.wait_ge(dve_rinv, c.n * 2 + 1)
                        nc.vector.tensor_reduce(sm[:, h, :], heads(pb[:, h, :]), AX_X, ALU.add)\
                            .then_inc(dve_sum, 1)
                        dve.wait_ge(dve_sum, c.n * 2 + (h + 1) + 1)
                        dve.wait_ge(pool_pn, c.n * 2 + 1)
                        nc.vector.reciprocal(rinv[:, h, :], sm[:, h, :]).then_inc(dve_rinv, 1)
                if a is not None:
                    cosine_and_sums(a, 2)
                    cosine_and_sums(a, 3)
                if f is not None:
                    dve.wait_ge(f_up, f.n + 2)
                    dve.wait_ge(f_gelu, f.n + 2)
                    dve.wait_ge(f_down, f.n + 1)
                    for k, (off, n) in enumerate(HCH):
                        last = nc.vector.scalar_tensor_tensor(hid[0:n, k, :], score[1][0:n, k * TILE:(k + 1) * TILE],
                                                              vec[0:n, 3 + k:4 + k], gate[0:n, k, :],
                                                              ALU.add, ALU.mult)
                    last.then_inc(f_hid, 1)
                if e is not None:
                    dve.wait_ge(f_var, e.n + 2)
                    nc.vector.tensor_scalar(sums[:, ROOTS - 1:ROOTS], tran[1][:, 0:1], EPS, None, ALU.add)\
                        .then_inc(f_eps, 1)
                    dve.wait_ge(f_eps, e.n + 2)
                    dve.wait_ge(f_spread, e.n + 1)
                if a is not None:
                    dve.wait_ge(dve_ssq, a.n * 4 + 4 + 1)
                    dve.wait_ge(pool_qk, a.n * 4 + 1)
                    w = ROOTS if e is not None else ROOTS - 1
                    inverse_root(dve, sums[:, 0:w], 1e-24, ALU.max, inv[:, 0:w], root_done, a.n * ROOT_STEPS + 1)
                    rotate(a, 2)
                    rotate(a, 3)
                elif e is not None:
                    inverse_root(dve, sums[:, ROOTS - 1:ROOTS], 1e-24, ALU.max, inv[:, ROOTS - 1:ROOTS], f_root,
                                 late_root(e, blk) * ROOT_STEPS + 1)
                if c is not None and c.first:
                    dve.wait_ge(pe_o, c.n * 2 + 1)
                    nc.vector.memset(vs[0:WINDOW, :, :], 0.0).then_inc(dve_vz, 1)
                if f is not None:
                    dve.wait_ge(f_down, f.n + 2)
                    xt = tile_of(xT, f.t)
                    nc.vector.scalar_tensor_tensor(xt, tran[0][:, 0:TILE], vec[:, 2:3], xt, ALU.add, ALU.add)\
                        .then_inc(f_x, 1)
                    dve.wait_ge(f_x, f.n + 2)
                    shift(xA, xT, f.t * TILE, TILE).then_inc(f_shift, 1)
            block_steps(dve, blk, step)

        def hold(pool):
            pool.sem_inc(pool_held, 1)

        def pool_block(pool, blk):
            def sine(a, i):
                pool.wait_ge(act_raw, a.n * 4 + (i + 1) + 1)
                pool.wait_ge(dve_rope, a.n * 4 + 1)
                tb = tab[:, i // 2 * 2 + 1, :]
                half = DH // 2
                hold(pool)
                for o in range(2):
                    last = nc.gpsimd.tensor_tensor(
                        heads(sinp[:, i, :])[:, :, o * half:(o + 1) * half],
                        heads(raw[:, i, :])[:, :, (1 - o) * half:(2 - o) * half],
                        over_heads(tb[:, o * half:(o + 1) * half], half), ALU.mult)
                last.then_inc(pool_sin, 1)

            def step(s, a, b, c, d, e, f):
                if a is not None:
                    pool.wait_ge(dve_cos, a.n * 4 + 1)
                    pool.wait_ge(pool_sin, a.n * 4 + 1)
                    trig_t = trig_sb[:, :, a.t, :] if isinstance(a.t, int) else \
                        trig_sb[:, :, bass.ds(a.t, 1), :].rearrange("p i a d -> p i (a d)")
                    scales_l = scales[:, a.l, :, :] if isinstance(a.l, int) else \
                        scales[:, bass.ds(a.l, 1), :, :].rearrange("p a i d -> p (a i) d")
                    hold(pool)
                    nc.gpsimd.tensor_tensor(tab[:, :, :], trig_t, scales_l, ALU.mult).then_inc(pool_tab, 1)
                    pool.wait_ge(pool_tab, a.n + 2)
                    sine(a, 0)
                    sine(a, 1)
                if c is not None:
                    for h in range(HALVES):
                        pool.wait_ge(dve_rinv, c.n * 2 + (h + 1) + 1)
                        hold(pool)
                        nc.gpsimd.tensor_tensor(heads(pb[:, h, :]), heads(pb[:, h, :]), per_head(rinv[:, h, :]),
                                                ALU.mult).then_inc(pool_pn, 1)
                if a is not None:
                    sine(a, 2)
                    sine(a, 3)
                    for i in range(4):
                        pool.wait_ge(dve_rope, a.n * 4 + (i + 1) + 1)
                        pool.wait_ge(root_done, (a.n + 1) * ROOT_STEPS + 1)
                        hold(pool)
                        nc.gpsimd.tensor_tensor(heads(qk[:, i, :]), heads(qk[:, i, :]), per_head(rnorm[:, i, :]),
                                                ALU.mult).then_inc(pool_qk, 1)
            block_steps(pool, blk, step)

        def layer_rows(w, l):
            return w[l, :, :] if isinstance(l, int) else w[bass.ds(l, 1), :, :].rearrange("a r c -> (a r) c")

        def load_qk(sp, l):
            w = layer_rows(w_qkv, l)
            sp.dma_start(wqkv[:, 0:PAIRS * P], w[:, 0:PAIRS * P]).then_inc(ld_q, 16)
            sp.dma_start(wqkv[:, PAIRS * P:2 * PAIRS * P], w[:, PAIRS * P:2 * PAIRS * P]).then_inc(ld_k, 16)

        def load_v(sp, l):
            sp.dma_start(wqkv[:, 2 * PAIRS * P:], layer_rows(w_qkv, l)[:, 2 * PAIRS * P:]).then_inc(ld_v, 16)

        def load_o(sp, l):
            sp.dma_start(wo[:, :, :], layer_rows(w_o, l).rearrange("(j r) c -> r j c", r=P)).then_inc(ld_o, 16)

        def load_ffn(sp, l):
            sp.dma_start(w1[:, :], layer_rows(w_1, l)).then_inc(ld_ffn, 16)
            rows = layer_rows(w_2, l)
            sp.dma_start(w2[:, 0:2, :], rows[0:256, :].rearrange("(k r) c -> r k c", r=P)).then_inc(ld_ffn, 16)
            sp.dma_start(w2[0:HIDDEN - 256, 2, :], rows[256:HIDDEN, :]).then_inc(ld_ffn, 16)
            sp.dma_start(vec[:, :], layer_rows(vecs, l)).then_inc(ld_ffn, 16)

        def sp_block(sp, blk):
            def step(s, a, b, c, d, e, f):
                new = isinstance(s, int) and not (blk == 0 and a is not None and isinstance(a.l, int)) \
                    and not (blk == 1 and (a is None or isinstance(a.l, int)))
                if new:
                    l = 0 if a is None else a.l
                    at = s % TILES
                    done = (DEPTH * (blk + 1) if a is None else a.L) * TILES
                    if at == 2:
                        sp.wait_ge(pe_v, done * 2 + 1)
                        load_v(sp, l)
                    if at == 3:
                        sp.wait_ge(pe_y, done + 1)
                        load_o(sp, l)
                if isinstance(s, int) and s == TILES - 1:
                    sp.wait_ge(pe_qk, (a.n + 1) * 4 + 1)
                    load_qk(sp, a.l + 1)
                if d is not None and not (isinstance(d.t, int) and d.t == TILES - 1):
                    sp.wait_ge(pe_o, d.n * 2 + 2 + 1)
                    sp.dma_start(vs[0:WINDOW, :, :], vt[P - WINDOW:P, :, :]).then_inc(v_carried, 16)
                if c is not None:
                    for h in range(HALVES):
                        sp.wait_ge(act_v, c.n * 2 + (h + 1) + 1)
                        sp.dma_start(vs[WINDOW:P, h, :], vt[0:P - WINDOW, h, :]).then_inc(v_moved[h], 16)
                if new and at == 4:
                    sp.wait_ge(f_down, done + 1)
                    sp.wait_ge(f_x, done + 1)
                    load_ffn(sp, l)
            block_steps(sp, blk, step, apart=True)

        def pe_norm(pe, blk):
            n = blk * CHUNKS
            if blk == 0:
                pe.wait_ge(ld_const, LOADS * 16)
                pe.wait_ge(pool_init, 1 + 1)
            elif blk == 1:
                pe.wait_ge(act_v, DEPTH * TILES * 2 + 1)
                pe.wait_ge(dve_y, DEPTH * TILES + 1)
            else:
                pe.wait_ge(c_x, TILES + 1)
            pe.wait_ge(n_x, n + 1)

            def var(j):
                pe.wait_ge(n_sq, n + j + 2)
                for m in range(BANK // P):
                    last = nc.tensor.matmul(outp[0][:, 4 * j + m:4 * j + m + 1], raw[:, j, m * P:(m + 1) * P],
                                            mean_w[:, 0:1], start=True, stop=True, skip_group_check=True)
                last.then_inc(n_var, 1)

            for j in range(CHUNKS):
                if blk == 1:
                    pe.wait_ge(h_x, j + 2)
                if j >= 2:
                    pe.wait_ge(n_xc, n + j - 1 + 1)
                nc.tensor.matmul(proj[j % 2][:, :], mean_w[:, :], xm[:, j * BANK:(j + 1) * BANK],
                                 start=True, stop=True).then_inc(n_mean, 1)
                if j >= 1:
                    var(j - 1)
            var(CHUNKS - 1)
            pe.wait_ge(n_root, (blk + 1) * ROOT_STEPS + 1)
            for j in range(CHUNKS):
                if j >= 2:
                    pe.wait_ge(n_x, n + j - 1 + 1)
                for m in range(BANK // P):
                    last = nc.tensor.matmul(proj[j % 2][:, m * P:(m + 1) * P],
                                            rstd[:, 4 * j + m:4 * j + m + 1].broadcast_to([P, P]),
                                            identf[:, :], start=True, stop=True, skip_group_check=True)
                last.then_inc(n_spread, 1)

        def act_norm(act, blk):
            for j in range(CHUNKS):
                act.wait_ge(n_xc, blk * CHUNKS + j + 2)
                nc.scalar.activation(raw[:, j, :], xT[:, j * BANK:(j + 1) * BANK], ACT.Square).then_inc(n_sq, 1)

        def dve_norm(dve, blk):
            n = blk * CHUNKS
            if blk == 1:
                dve.wait_ge(h_x, CHUNKS + 1)
            for j in range(CHUNKS):
                s = slice(j * BANK, (j + 1) * BANK)
                dve.wait_ge(n_mean, n + j + 2)
                nc.vector.tensor_tensor(xT[:, s], xm[:, s], proj[j % 2][:, :], ALU.subtract).then_inc(n_xc, 1)
            dve.wait_ge(n_var, n + CHUNKS + 1)
            inverse_root(dve, outp[0][:, 0:TILES], EPS, ALU.add, rstd[:, :], n_root, blk * ROOT_STEPS + 1)
            for j in range(CHUNKS):
                s = slice(j * BANK, (j + 1) * BANK)
                dve.wait_ge(n_spread, n + j + 2)
                nc.vector.tensor_tensor(xT[:, s], xT[:, s], proj[j % 2][:, :], ALU.mult).then_inc(n_x, 1)
                if blk != 1:
                    dve.wait_ge(n_x, n + j + 2)
                    shift(xA, xT, j * BANK, BANK).then_inc(n_shift, 1)

        def dve_half_step(dve, blk):
            dve.wait_ge(f_x, (blk + 1) * DEPTH * TILES + 1)
            for j in range(CHUNKS):
                s = slice(j * BANK, (j + 1) * BANK)
                nc.vector.scalar_tensor_tensor(xm[:, s], xT[:, s], 0.5, xm[:, s], ALU.mult, ALU.add)\
                    .then_inc(h_x, 1)

        qT2 = xA[:, 0:T]
        kT2 = xB[:, 0:T]
        v2 = v_area[:, :, :].rearrange("p a (t d) -> p (a t) d", d=P)
        p2 = sb("p2", [P, 2, T])
        pt2 = qk[:, :, :].rearrange("p a (t d) -> p (a t) d", d=P)
        st = sb("st", [P, 2, 4])
        on2 = sb("on2", [P, P])
        sbank = banks[4:8]
        tbank = banks[2:4]
        A_SCALE = float(P) ** -0.5
        NQ = 3 * CHUNKS
        NV = TILES // 4

        def groups(i):
            return [(g, min(4, i + 1 - 4 * g)) for g in range(i // 4 + 1)]

        GBASE = [sum(len(groups(m)) for m in range(i)) for i in range(TILES + 1)]

        def pe_causal(pe):
            pe.wait_ge(n_x, 2 * CHUNKS + 1)
            for n in range(NQ + NV):
                if n >= 2:
                    pe.wait_ge(c_evac, n - 1 + 1)
                if n >= NQ:
                    pe.wait_ge(c_evac, n - NV + 2)
                if n < NQ:
                    kind, j = divmod(n, CHUNKS)
                    last = nc.tensor.matmul(proj[n % 2][:, :], awqkv[:, kind * P:(kind + 1) * P],
                                            xT[:, j * BANK:(j + 1) * BANK], start=True, stop=True)
                else:
                    for m in range(4):
                        last = nc.tensor.matmul(proj[n % 2][:, m * P:(m + 1) * P],
                                                raw[:, n - NQ, m * P:(m + 1) * P], awproj[:, :],
                                                start=True, stop=True, skip_group_check=True)
                last.then_inc(c_proj, 1)
            pe.wait_ge(c_evac, NQ + NV + 1)

            def scores(i):
                if i >= 1:
                    pe.wait_ge(c_exp, i + 1)
                for g, m in groups(i):
                    diag = g == i // 4
                    last = nc.tensor.matmul(sbank[g][:, 0:m * P], qT2[:, i * P:(i + 1) * P],
                                            kT2[:, g * BANK:g * BANK + m * P], start=True, stop=not diag,
                                            skip_group_check=True)
                    if diag:
                        last = nc.tensor.matmul(sbank[g][:, (m - 1) * P:m * P], identb[:, :], causalb[:, :],
                                                start=False, stop=True, skip_group_check=True)
                last.then_inc(c_s, 1)

            def transposed_output(i):
                pe.wait_ge(c_on, i + 2)
                pe.wait_ge(c_x, i + 1)
                nc.tensor.transpose(proj[1][:, 0:P], on2[:, :], identf[:, :]).then_inc(c_ot, 1)

            scores(0)
            for i in range(TILES):
                pe.wait_ge(c_exp, i + 2)
                if i + 1 < TILES:
                    scores(i + 1)
                for g, m in groups(i):
                    n = GBASE[i] + g
                    if n >= 2:
                        pe.wait_ge(c_pt, n - 1 + 1)
                    for e in range(m):
                        last = nc.tensor.transpose(tbank[n % 2][:, e * P:(e + 1) * P],
                                                   p2[:, i % 2, (4 * g + e) * P:(4 * g + e + 1) * P], identf[:, :])
                    last.then_inc(c_t, 1)
                if i >= 1:
                    transposed_output(i - 1)
                for g, m in groups(i):
                    pe.wait_ge(c_pt, GBASE[i] + g + 2)
                    for e in range(m):
                        t = 4 * g + e
                        last = nc.tensor.matmul(proj[0][:, 0:P], pt2[:, t, :], v2[:, t, :],
                                                start=(t == 0), stop=(t == i))
                last.then_inc(c_o, 1)
            transposed_output(TILES - 1)

        def act_causal(act):
            for n in range(NQ + NV):
                act.wait_ge(c_proj, n + 2)
                if n < NQ:
                    kind, j = divmod(n, CHUNKS)
                    dst = raw[:, j, :] if kind == 2 else (qT2, kT2)[kind][:, j * BANK:(j + 1) * BANK]
                else:
                    dst = v2[:, (n - NQ) * 4:(n - NQ) * 4 + 4, :].rearrange("p t d -> p (t d)")
                nc.scalar.activation(dst, proj[n % 2][:, :], ACT.Copy).then_inc(c_evac, 1)
            for i in range(TILES):
                act.wait_ge(c_neg, i + 2)
                if i >= 2:
                    act.wait_ge(c_o, i - 1 + 1)
                n = (i + 1) * P
                view = [(g, m) for g, m in groups(i)]
                for g, m in view:
                    last = nc.scalar.activation(p2[:, i % 2, g * BANK:g * BANK + m * P], sbank[g][:, 0:m * P],
                                                ACT.Exp, bias=st[:, i % 2, 1:2], scale=A_SCALE,
                                                accum_out=part[:, i % 2, g:g + 1])
                last.then_inc(c_exp, 1)

        mask32 = p2[:, 0, 0:3 * P].rearrange("p (a k) -> p a k", k=P)
        part = sb("part", [P, 2, 4])
        gmax = sb("gmax", [P, 2, 4])
        c_gmax, c_sum = sem("c_gmax"), sem("c_sum")

        def dve_causal(dve):
            def maxima(i):
                dve.wait_ge(c_s, i + 2)
                k = len(groups(i))
                for g, m in groups(i):
                    nc.vector.tensor_reduce(gmax[:, i % 2, g:g + 1], sbank[g][:, 0:m * P], AX_X, ALU.max)\
                        .then_inc(c_gmax, 1)
                dve.wait_ge(c_gmax, GBASE[i + 1] + 1)
                nc.vector.tensor_reduce(st[:, i % 2, 0:1], gmax[:, i % 2, 0:k], AX_X, ALU.max).then_inc(c_max, 1)
                dve.wait_ge(c_max, i + 2)
                nc.vector.tensor_scalar(st[:, i % 2, 1:2], st[:, i % 2, 0:1], -A_SCALE, None, ALU.mult)\
                    .then_inc(c_neg, 1)

            def add_output(i):
                dve.wait_ge(c_ot, i + 2)
                s = slice(i * P, (i + 1) * P)
                nc.vector.tensor_tensor(xm[:, s], proj[1][:, 0:P], xm[:, s], ALU.add).then_inc(c_x, 1)

            maxima(0)
            for i in range(TILES):
                dve.wait_ge(c_exp, i + 2)
                k = len(groups(i))
                nc.vector.tensor_reduce(st[:, i % 2, 2:3], part[:, i % 2, 0:k], AX_X, ALU.add).then_inc(c_sum, 1)
                dve.wait_ge(c_sum, i + 2)
                nc.vector.reciprocal(st[:, i % 2, 3:4], st[:, i % 2, 2:3]).then_inc(c_inv, 1)
                if i + 1 < TILES:
                    maxima(i + 1)
                for g, m in groups(i):
                    dve.wait_ge(c_t, GBASE[i] + g + 2)
                    if i >= 1:
                        dve.wait_ge(c_o, i + 1)
                    nc.vector.tensor_copy(pt2[:, 4 * g:4 * g + m, :].rearrange("p t q -> p (t q)"),
                                          tbank[(GBASE[i] + g) % 2][:, 0:m * P]).then_inc(c_pt, 1)
                if i >= 1:
                    add_output(i - 1)
                dve.wait_ge(c_o, i + 2)
                dve.wait_ge(c_inv, i + 2)
                nc.vector.tensor_scalar(on2[:, :], proj[0][:, 0:P], st[:, i % 2, 3:4], None, ALU.mult)\
                    .then_inc(c_on, 1)
            add_output(TILES - 1)

        LOADS = 9

        PE_SEMS = [pe_tq, pe_tk, pe_tp, pe_qk, pe_v, pe_s, pe_o, pe_y, f_mean, f_var, f_spread, f_gate, f_up,
                   f_down, n_mean, n_var, n_spread, c_proj, c_s, c_t, c_o, c_ot]
        ACT_SEMS = [act_xq, act_xv, act_qz, act_kt, act_pt, act_raw, act_sq, act_v, act_exp, act_o, f_sq, f_gelu, n_sq, c_evac,
                    c_exp]
        DVE_SEMS = [dve_ssq, dve_cos, dve_rope, dve_halo, dve_max, dve_sub, dve_sum, dve_rinv, dve_y,
                    dve_xb, dve_vz, f_eps, dve_zero, root_done, f_root, n_root, f_xc, f_xh, f_xn, f_hid, f_x, f_shift, n_xc, n_x,
                    n_shift, h_x, c_max, c_neg, c_inv, c_pt, c_on, c_x, c_gmax, c_sum]
        POOL_SEMS = [pool_sin, pool_qk, pool_pn, pool_tab, pool_init]

        def start_at_one(eng, sems):
            for s in sems:
                eng.sem_inc(s, 1)

        block = ctx.enter_context(nc.Block())

        @block.sync
        def _(sp):
            sp.dma_start(xm[:, :], x_t).then_inc(ld_const, 16)
            sp.dma_start(identf[:, :], ident).then_inc(ld_const, 16)
            sp.dma_start(mask32[:, 0:2, :], mask).then_inc(ld_const, 16)
            sp.dma_start(mask32[:, 2, :], causal).then_inc(ld_const, 16)
            sp.dma_start(reb[:, :], rebase).then_inc(ld_const, 16)
            sp.dma_start(awqkv[:, :], a_wqkv).then_inc(ld_const, 16)
            sp.dma_start(awproj[:, :], a_wproj).then_inc(ld_const, 16)
            sp.dma_start(trig_sb[:, :, :, :], trig).then_inc(ld_const, 16)
            sp.dma_start(scales[:, :, :, :], qk_scales.rearrange("(o l) i d -> o (l i d)", o=1)
                         .broadcast_to([P, DEPTH * 4 * DH]).rearrange("p (l i d) -> p l i d", i=4, d=DH))\
                .then_inc(ld_const, 16)
            load_qk(sp, 0)
            load_v(sp, 0)
            load_o(sp, 0)
            load_ffn(sp, 0)
            for blk in range(2):
                sp_block(sp, blk)
            sp.wait_ge(ld_q, (2 * DEPTH + 1) * 16)
            sp.wait_ge(ld_k, (2 * DEPTH + 1) * 16)
            for j in range(CHUNKS):
                sp.wait_ge(h_x, CHUNKS + j + 2)
                sp.dma_start(out_t[:, j * BANK:(j + 1) * BANK], xm[:, j * BANK:(j + 1) * BANK]).then_inc(out_done, 16)
            sp.wait_ge(out_done, CHUNKS * 16)

        @block.gpsimd
        def _(pool):
            start_at_one(pool, POOL_SEMS)
            nc.gpsimd.memset(mean_w[:, :], 1.0 / P)
            nc.gpsimd.memset(qz[:, :, :, :, :], 0.0)
            nc.gpsimd.memset(pT[:, :, :, :, :, :], 0.0).then_inc(pool_init, 1)
            pool.wait_ge(ld_const, LOADS * 16)
            for blk in range(2):
                pool.wait_ge(n_shift, (blk + 1) * CHUNKS + 1)
                pool_block(pool, blk)

        @block.scalar
        def _(act):
            start_at_one(act, ACT_SEMS)
            act_norm(act, 0)
            act.wait_ge(pool_init, 1 + 1)
            for blk in range(2):
                act_block(act, blk)
                if blk == 0:
                    act_norm(act, 1)
                    act_causal(act)
                    act_norm(act, 2)

        @block.vector
        def _(dve):
            start_at_one(dve, DVE_SEMS)
            def no_token_before():
                nc.vector.memset(xA[64:P, 0:1], 0.0)
                nc.vector.memset(xB[64:P, 0:1], 0.0).then_inc(dve_zero, 1)

            no_token_before()
            dve.wait_ge(ld_const, LOADS * 16)
            nc.vector.tensor_copy(identb[:, :], identf[:, :])
            nc.vector.tensor_copy(causalb[:, :], mask32[:, 2, :])
            nc.vector.tensor_copy(maskb[:, :, :], mask32[:, 0:2, :]).then_inc(dve_masks, 1)
            dve_norm(dve, 0)
            for blk in range(2):
                dve_block(dve, blk)
                dve_half_step(dve, blk)
                if blk == 0:
                    dve_norm(dve, 1)
                    dve_causal(dve)
                    no_token_before()
                    dve_norm(dve, 2)

        @block.tensor
        def _(pe):
            start_at_one(pe, PE_SEMS)
            pe_norm(pe, 0)
            pe.wait_ge(dve_masks, 1)
            for blk in range(2):
                pe_block(pe, blk)
                if blk == 0:
                    pe_norm(pe, 1)
                    pe_causal(pe)
                    pe_norm(pe, 2)


def _constants(T):
    import numpy as np
    half = np.arange(0, DH, 2, dtype=np.float32)
    inv_freq = (np.float32(1.0) / np.power(np.float32(10000.0), half / np.float32(DH))).astype(np.float32)
    t = np.arange(T, dtype=np.float32)
    ang = (t[:, None] * inv_freq[None, :]).astype(np.float32).astype(np.float64)
    ang = np.concatenate([ang, ang], -1)
    base = ((half + 0.4 * DH) / (1.4 * DH)).astype(np.float32).astype(np.float64)
    base = np.concatenate([base, base])
    power = (np.arange(T) % TILE - TILE // 2) / (WINDOW // 2)
    scale = base[None, :] ** power[:, None]
    sign = np.where(np.arange(DH) < DH // 2, -1.0, 1.0)[None, :]
    tabs = np.stack([np.cos(ang) * scale, sign * np.sin(ang) * scale, np.cos(ang) / scale, sign * np.sin(ang) / scale])
    trig = tabs.reshape(4, T // TILE, TILE, DH).transpose(2, 0, 1, 3).astype(np.float32)
    rebase = np.tile(base ** (TILE / (WINDOW // 2)), 2)[:, None].astype(np.float32)
    q = np.arange(P) % WINDOW
    wl = np.arange(P) // 64
    j = np.arange(P) % 64
    u = np.arange(P) // 64
    band = (j[None, :] >= q[:, None]) & (j[None, :] <= q[:, None] + WINDOW)
    start = band & ~((wl[:, None] == 0) & (u[None, :] == 0) & (j[None, :] < WINDOW))
    mask = np.where(np.stack([start, band], 1), 0.0, -1e30).astype(np.float32)
    ident = np.eye(P, dtype=np.float32)
    causal = np.where(np.arange(P)[:, None] >= np.arange(P)[None, :], 0.0, -1e30).astype(np.float32)
    return trig, rebase, mask, ident, causal


def kernel(**inputs):
    import numpy as np
    import concourse.bacc as bacc
    from concourse import mybir as mb
    from concourse.bass_utils import run_bass_kernel_spmd as run

    g = {k: np.asarray(v) for k, v in inputs.items()}
    x = g["L0_attn_x"]
    T = x.shape[1]
    trig, rebase, mask, ident, causal = _constants(T)

    def swap(a):
        return np.concatenate([a[:, DH // 2:], a[:, :DH // 2]], 1)

    qs, ks = g["L0_ffn_q_scale"], g["L0_ffn_k_scale"]
    scales = np.stack([qs, swap(qs), ks, swap(ks)], 1)
    vecs = np.zeros((DEPTH, P, 9), np.float32)
    for i, name in enumerate(("L0_ffn_ln_g", "L0_ffn_ln_b", "L0_ffn_b2")):
        vecs[:, :, i] = g[name]
    b1 = g["L0_ffn_b1"]
    for k, (off, n) in enumerate(HCH):
        vecs[:, :n, 3 + k] = b1[:, off:off + n]
        vecs[:, :n, 6 + k] = b1[:, HIDDEN + off:HIDDEN + off + n]
    arrays = {
        "x_t": x[0].T, "w_qkv": np.concatenate([g["L0_ffn_Wqkv"], g["L0_ffn_Wqkv"][:1]], 0), "w_o": g["L0_ffn_Wo"],
        "w_1": g["L0_ffn_W1"], "w_2": g["L0_ffn_W2"], "vecs": vecs, "qk_scales": scales, "trig": trig,
        "rebase": rebase, "mask": mask, "ident": ident, "causal": causal,
        "a_wqkv": g["L0_attn_Wqkv"], "a_wproj": g["L0_attn_Wproj"],
    }
    arrays = {k: np.ascontiguousarray(v) for k, v in arrays.items()}
    nc = bacc.Bacc("TRN2", target_bir_lowering=False, num_devices=1)
    ap = {k: nc.dram_tensor(k + "_dram", v.shape, mb.dt.from_np(v.dtype), kind="ExternalInput").ap() for k, v in arrays.items()}
    out = nc.dram_tensor("out_t_dram", (P, T), mb.dt.float32, kind="ExternalOutput").ap()
    bass_macaron(nc, ap["x_t"], ap["w_qkv"], ap["w_o"], ap["w_1"], ap["w_2"], ap["vecs"], ap["qk_scales"],
                 ap["trig"], ap["rebase"], ap["mask"], ap["ident"], ap["causal"],
                 ap["a_wqkv"], ap["a_wproj"], out)
    r = run(nc, [{k + "_dram": v for k, v in arrays.items()}], core_ids=[0])
    return np.ascontiguousarray(r.results[0]["out_t_dram"].T)[None]
```
